# Optimizing a Trainium2 kernel written in Bass

```python
import numpy as np
import jax
import jax.numpy as jnp

def _softmax(x, axis=-1):
    return jax.nn.softmax(x, axis=axis)

def _gelu(x):
    return jax.nn.gelu(x, approximate=True)

def _silu(x):
    return jax.nn.silu(x)

def _sigmoid(x):
    return jax.nn.sigmoid(x)

def _layernorm(x, axis=-1, eps=1e-05):
    m = jnp.mean(x, axis=axis, keepdims=True)
    v = jnp.var(x, axis=axis, keepdims=True)
    return (x - m) / jnp.sqrt(v + eps)

def _scatter_add(tgt, idx, src, axis=0):
    return tgt.at[idx].add(src)

def _segment_sum(src, seg, n):
    return jax.ops.segment_sum(src, seg, n)
kernel_name = 'mk_adaln_d1_jaxref_r4_1a3681'

def setup_inputs(seed: int=0):
    np.random.seed(seed)
    _w = jnp.asarray

    def _L0_attn_setup():
        import jax, jax.numpy as jnp
        import numpy as np
        DIM = 256
        NUM_HEADS = 16
        DIM_HEAD = DIM // NUM_HEADS
        NORM = DIM_HEAD ** (-0.5)
        key = jax.random.key(seed)
        k0, k1, k2, k3 = jax.random.split(key, 4)
        B, N = (2, 512)
        x = jax.random.normal(k0, (B, N, DIM), dtype=jnp.float32)
        Wq = jax.random.normal(k1, (NUM_HEADS, DIM_HEAD, DIM_HEAD), dtype=jnp.float32) * DIM_HEAD ** (-0.5)
        Wp = jax.random.normal(k2, (DIM, DIM), dtype=jnp.float32) * DIM ** (-0.5)
        bp = jax.random.normal(k3, (DIM,), dtype=jnp.float32) * 0.01
        return {'x': x, 'Wq': Wq, 'Wp': Wp, 'bp': bp}
    _L0_attn_in = _L0_attn_setup()

    def _L0_ffn_setup():
        import jax, jax.numpy as jnp
        import numpy as np
        B, S, H, F, G = (8, 512, 256, 1024, 128)
        EPS = 1e-05

        def _dequant(q, scales, g):
            K, N = q.shape
            w = (q.astype(jnp.float32) - 128.0).reshape(K // g, g, N) * scales[:, None, :]
            return w.reshape(K, N)
        key = jax.random.key(seed)
        ks = jax.random.split(key, 8)
        x = jax.random.normal(ks[0], (B, S, H), dtype=jnp.float32)
        ln_gamma = jnp.ones((H,), jnp.float32)
        ln_beta = jnp.zeros((H,), jnp.float32)
        fc1_q = jax.random.randint(ks[1], (H, F), 0, 64, dtype=jnp.int32)
        fc2_q = jax.random.randint(ks[2], (F, H), 0, 64, dtype=jnp.int32)
        fc1_scales = jax.random.uniform(ks[3], (H // G, F), jnp.float32) * 0.02 + 0.001
        fc2_scales = jax.random.uniform(ks[4], (F // G, H), jnp.float32) * 0.02 + 0.001
        fc1_bias = jax.random.normal(ks[5], (F,), jnp.float32) * 0.02
        fc2_bias = jax.random.normal(ks[6], (H,), jnp.float32) * 0.02
        return {'x': x, 'ln_gamma': ln_gamma, 'ln_beta': ln_beta, 'fc1_q': fc1_q, 'fc1_scales': fc1_scales, 'fc1_bias': fc1_bias, 'fc2_q': fc2_q, 'fc2_scales': fc2_scales, 'fc2_bias': fc2_bias}
    _L0_ffn_in = _L0_ffn_setup()
    _L0_c = _w((lambda *s: np.random.randn(*s).astype(np.float32) * 0.05)(1, 256))
    _L0_wmod = _w((lambda *s: np.random.randn(*s).astype(np.float32) * 0.05)(256, 6 * 256) * 256 ** (-0.5))
    _d = {'L0_attn_x': _L0_attn_in['x'], 'L0_attn_Wq': _L0_attn_in['Wq'], 'L0_attn_Wp': _L0_attn_in['Wp'], 'L0_attn_bp': _L0_attn_in['bp'], 'L0_ffn_ln_gamma': _L0_ffn_in['ln_gamma'], 'L0_ffn_ln_beta': _L0_ffn_in['ln_beta'], 'L0_ffn_fc1_q': _L0_ffn_in['fc1_q'], 'L0_ffn_fc1_scales': _L0_ffn_in['fc1_scales'], 'L0_ffn_fc1_bias': _L0_ffn_in['fc1_bias'], 'L0_ffn_fc2_q': _L0_ffn_in['fc2_q'], 'L0_ffn_fc2_scales': _L0_ffn_in['fc2_scales'], 'L0_ffn_fc2_bias': _L0_ffn_in['fc2_bias'], 'L0_c': _L0_c, 'L0_wmod': _L0_wmod}
    _x0 = _d['L0_attn_x']
    _d['L0_attn_x'] = jax.random.normal(jax.random.fold_in(jax.random.key(seed), 1), (1, 4096, 256), dtype=_x0.dtype)
    del _x0
    return _d

def reference(L0_attn_x, L0_attn_Wq, L0_attn_Wp, L0_attn_bp, L0_ffn_ln_gamma, L0_ffn_ln_beta, L0_ffn_fc1_q, L0_ffn_fc1_scales, L0_ffn_fc1_bias, L0_ffn_fc2_q, L0_ffn_fc2_scales, L0_ffn_fc2_bias, L0_c, L0_wmod):

    def _L0_attn_ref(x, Wq, Wp, bp):
        import jax, jax.numpy as jnp
        import numpy as np
        DIM = 256
        NUM_HEADS = 16
        DIM_HEAD = DIM // NUM_HEADS
        NORM = DIM_HEAD ** (-0.5)
        B, N, D = x.shape
        xh = x.reshape(B, N, NUM_HEADS, DIM_HEAD)
        q = jnp.einsum('bnhd,hed->bnhe', xh, Wq)
        scores = jnp.einsum('bnhe,bmhe->bhnm', q, q)
        scores = scores / NORM
        attn = jax.nn.softmax(scores, axis=-1)
        res = jnp.einsum('bhnm,bmhe->bnhe', attn, q)
        y = res.reshape(B, N, D)
        y = y @ Wp.T + bp
        return y

    def _L0_ffn_ref(x, ln_gamma, ln_beta, fc1_q, fc1_scales, fc1_bias, fc2_q, fc2_scales, fc2_bias):
        import jax, jax.numpy as jnp
        import numpy as np
        B, S, H, F, G = (8, 512, 256, 1024, 128)
        EPS = 1e-05

        def _dequant(q, scales, g):
            K, N = q.shape
            w = (q.astype(jnp.float32) - 128.0).reshape(K // g, g, N) * scales[:, None, :]
            return w.reshape(K, N)
        residual = x
        mu = jnp.mean(x, axis=-1, keepdims=True)
        var = jnp.mean(jnp.square(x - mu), axis=-1, keepdims=True)
        h = (x - mu) * jax.lax.rsqrt(var + EPS) * ln_gamma + ln_beta
        hf = h.reshape(-1, H)
        w1 = _dequant(fc1_q, fc1_scales, G)
        y = hf @ w1 + fc1_bias
        y = jax.nn.silu(y)
        w2 = _dequant(fc2_q, fc2_scales, G)
        z = y @ w2 + fc2_bias
        return residual + 0.5 * z.reshape(residual.shape)
    x = L0_attn_x
    mod = (_silu(L0_c) @ L0_wmod).reshape(L0_c.shape[0], 6, 1, -1)
    sa, ca, ga, sb, cb, gb = (mod[:, 0], mod[:, 1], mod[:, 2], mod[:, 3], mod[:, 4], mod[:, 5])
    ga = (2 * (ga >= 0) - 1) * jnp.maximum(jnp.abs(ga), 0.25)
    gb = (2 * (gb >= 0) - 1) * jnp.maximum(jnp.abs(gb), 0.25)
    h = _layernorm(x, axis=-1) * (1 + ca) + sa
    x = x + ga * _L0_attn_ref(h, L0_attn_Wq, L0_attn_Wp, L0_attn_bp)
    h = _layernorm(x, axis=-1) * (1 + cb) + sb
    x = x + gb * _L0_ffn_ref(h, L0_ffn_ln_gamma, L0_ffn_ln_beta, L0_ffn_fc1_q, L0_ffn_fc1_scales, L0_ffn_fc1_bias, L0_ffn_fc2_q, L0_ffn_fc2_scales, L0_ffn_fc2_bias)
    return x

_drawn_inputs = setup_inputs


def setup_inputs(seed=0):
    import zlib

    import numpy as np

    out = dict(_drawn_inputs(seed))
    spreads = {'L0_ffn_ln_gamma': (1.0, 0.2), 'L0_ffn_ln_beta': (0.0, 0.1)}
    factors = {'L0_attn_bp': 50.467, 'L0_ffn_fc1_bias': 64.0, 'L0_ffn_fc2_bias': 64.0}
    for name, (base, spread) in spreads.items():
        noise = np.random.default_rng([zlib.crc32(name.encode()), seed]).standard_normal(out[name].shape)
        drawn = base * np.exp(spread * noise) if base else spread * noise
        out[name] = jnp.asarray(drawn.astype(out[name].dtype))
    for name, factor in factors.items():
        out[name] = (out[name] * factor).astype(out[name].dtype)
    return out
```

```python
from contextlib import ExitStack

import concourse.bass as bass
from concourse import mybir

F32, BF16, I32 = mybir.dt.float32, mybir.dt.bfloat16, mybir.dt.int32
ALU = mybir.AluOpType
ACT = mybir.ActivationFunctionType
AX = mybir.AxisListType

P = 128
BANK = 512
N, D = 4096, 256
H, E = 16, 16
F = 1024
EPS = 1e-5
TILES = N // P
DC = D // P
FT = F // P
GT = BANK // P
G = N // BANK
ROWS = 6 * E
STACK = ROWS + 3
NCH = H * G
PAIRS = TILES // 2
UNITS = TILES // 4
S_RING, P_RING, LAG = 3, 8, 2
REACH = 120.0


class Scope:

    def __init__(self, ctx, nc, stage):
        self.nc, self.stage, self.stack = nc, stage, ctx.enter_context(ExitStack())

    def take(self, name, words):
        return self.stack.enter_context(self.nc.sbuf_tensor(f"{self.stage}_{name}", [P, words], F32))[:, :]

    def banks(self, name, n):
        return self.stack.enter_context(self.nc.psum_tensor(f"{self.stage}_{name}", [P, n, BANK], F32))[:, :, :]

    def close(self):
        self.stack.close()


def wait(eng, semaphore, value):
    if not isinstance(value, int) or value > 0:
        eng.wait_ge(semaphore, value)


def rounds(eng, body, n):
    body(0)
    with eng.Fori(1, n) as i:
        body(i)


RSQRT_STEPS = 12


def rsqrt(dve, y, v, work, step, n):
    shifted, square = work[:, 0, :], work[:, 1, :]
    v_eps = work[:, 2, :]
    k = n * RSQRT_STEPS
    dve.tensor_scalar(v_eps, v, EPS, None, ALU.add).then_inc(step, 1)
    dve.wait_ge(step, k + 1)
    dve.tensor_scalar(shifted.bitcast(I32), v_eps.bitcast(I32), 1, None, ALU.logical_shift_right).then_inc(step, 1)
    dve.wait_ge(step, k + 2)
    dve.tensor_scalar(y.bitcast(I32), shifted.bitcast(I32), -1.0, float(0x5F3759DF), ALU.mult, ALU.add).then_inc(step, 1)
    for i in range(3):
        dve.wait_ge(step, k + (3 + 3 * i))
        dve.tensor_tensor(square, y, y, ALU.mult).then_inc(step, 1)
        dve.wait_ge(step, k + (4 + 3 * i))
        dve.scalar_tensor_tensor(out=square, in0=square, scalar=-0.5, in1=v_eps, op0=ALU.mult, op1=ALU.mult).then_inc(step, 1)
        dve.wait_ge(step, k + (5 + 3 * i))
        dve.scalar_tensor_tensor(out=y, in0=square, scalar=1.5, in1=y, op0=ALU.add, op1=ALU.mult).then_inc(step, 1)
    dve.wait_ge(step, k + RSQRT_STEPS)


def adaln_layer(nc, x, wq_t, wp_t, bp, gamma, beta, fc1_q, fc1_s, fc1_b, fc2_q, fc2_s, fc2_b,
                c_in, wmod, eye, out):
    ctx = ExitStack()

    def sb(name, shape, dt=F32):
        return ctx.enter_context(nc.sbuf_tensor(name, shape, dt))

    def sem(name):
        return ctx.enter_context(nc.semaphore(name))

    with ctx:
        parts_dram = nc.dram_tensor("parts_dram", [3, D, N], BF16, kind="Internal").ap()
        shift_dram = nc.dram_tensor("shift_dram", [3, H, N], BF16, kind="Internal").ap()

        ident = sb("ident", [P, P])
        values = sb("values", [P, TILES, D])
        att = sb("att", [P, TILES, D])
        w1 = sb("w1", [P, DC, F])
        w2 = sb("w2", [P, FT, D])
        wp = sb("wp", [P, DC, D])
        mod = sb("mod", [P, 6, D])
        mod_col = sb("mod_col", [P, 4])
        bp_ga = sb("bp_ga", [P, D])
        b2_gb = sb("b2_gb", [P, D])
        gamma_col = sb("gamma_col", [P, DC])
        beta_col = sb("beta_col", [P, DC])
        b1_col = sb("b1_col", [P, FT])
        norms = sb("norms", [P, TILES, H])
        shifts = sb("shifts", [P, TILES, H])
        carried = sb("carried", [P, 2])

        def carry(pool):
            pool.tensor_tensor(carried[:, 1:2], ident[:, 0:1], ident[:, 0:1], ALU.mult)


        a = Scope(ctx, nc, "start")
        wmod_sb = a.take("wmod_sb", DC * 6 * D).rearrange("p (k m) -> p k m", k=DC)
        w1_int = a.take("w1_int", DC * F).bitcast(I32).rearrange("p (k f) -> p k f", k=DC)
        w1_scale = a.take("w1_scale", DC * F).rearrange("p (k f) -> p k f", k=DC)
        w2_int = a.take("w2_int", FT * D).bitcast(I32).rearrange("p (k f) -> p k f", k=FT)
        w2_scale = a.take("w2_scale", FT * D).rearrange("p (k f) -> p k f", k=FT)
        x_in = a.take("x_in", TILES * D).rearrange("p (t d) -> p t d", d=D)
        z_tok = a.take("z_tok", GT * D).rearrange("p (t d) -> p t d", t=GT)
        h_feat = a.take("h_feat", DC * BANK).rearrange("p (k n) -> p k n", k=DC)
        q_parts = a.take("q_parts", 3 * DC * BANK // 2).bitcast(BF16).rearrange("p (s k n) -> p s k n", s=3, k=DC)
        q_rest = a.take("q_rest", DC * BANK).rearrange("p (k n) -> p k n", k=DC)
        q_sq = a.take("q_sq", GT * D)
        wq_diag = a.take("wq_diag", DC * P).rearrange("p (k m) -> p k m", k=DC)
        silu_c = a.take("silu_c", 4 * DC).rearrange("p (s k) -> p s k", s=4)
        silu_wide = a.take("silu_wide", DC * P).rearrange("p (k m) -> p k m", k=DC)
        ones = a.take("ones", P)
        stats = a.take("stats", GT * 6).rearrange("p (t s) -> p t s", t=GT)
        moments = a.take("moments", GT * 2).rearrange("p (t s) -> p t s", t=GT)
        rstd = a.take("rstd", GT)
        rsqrt_work = a.take("rsqrt_work", 3 * GT).rearrange("p (s t) -> p s t", s=3)
        carrier = a.take("carrier", 1)
        sign = a.take("sign", 2 * D).rearrange("p (s d) -> p s d", s=2)
        negated = a.take("negated", 2 * D).rearrange("p (s d) -> p s d", s=2)

        x_v = x[0].rearrange("(t p) d -> p t d", p=P)
        out_v = out[0].rearrange("(t p) d -> p t d", p=P)

        const_in, c_loaded, wmod_in, weights_in = sem("const_in"), sem("c_loaded"), sem("wmod_in"), sem("weights_in")
        wq_in, x0_loaded, x_loaded, diag_zero = sem("wq_in"), sem("x0_loaded"), sem("x_loaded"), sem("diag_zero")
        c_exp, c_step, wide_ready, mod_mm, mod_copied = sem("c_exp"), sem("c_step"), sem("wide_ready"), sem("mod_mm"), sem("mod_copied")
        col_mm, col_ready, mod_step, w_step = sem("col_mm"), sem("col_ready"), sem("mod_step"), sem("w_step")
        stats_done, moments_done, rstd_done, z_ready = sem("stats_done"), sem("moments_done"), sem("rstd_done"), sem("z_ready")
        z_turned, h_ready, q_feat_mm, q_tok_mm = sem("z_turned"), sem("h_ready"), sem("q_feat_mm"), sem("q_tok_mm")
        part_a, rest_ab, part_b, part_c, parts_stored = sem("part_a"), sem("rest_ab"), sem("part_b"), sem("part_c"), sem("parts_stored")
        v_copied, sq_ready, norms_ready = sem("v_copied"), sem("sq_ready"), sem("norms_ready")

        ps_turn = a.banks("turn", 2)
        ps_qf = a.banks("q_feat", 2)
        ps_qt = a.banks("q_tok", 2)
        ps_mod = a.banks("mod", 1)[:, 0, :]
        ps_col = a.banks("col", 1)[:, 0, 0:4]

        with nc.Block() as block:

            @block.sync
            def _(sp):
                sp.dma_start(silu_c[:, 0, :], c_in).then_inc(c_loaded, 16)
                sp.dma_start(wmod_sb, wmod.rearrange("(k p) m -> p k m", p=P)).then_inc(wmod_in, 16)
                sp.dma_start(x_in[:, 0:GT, :], x_v[:, 0:GT, :]).then_inc(x0_loaded, 16)
                sp.dma_start(ident[:, :], eye).then_inc(const_in, 16)
                sp.wait_ge(diag_zero, 1)
                for h in range(H):
                    k, r = divmod(h, H // DC)
                    sp.dma_start(wq_diag[E * r:E * r + E, k, E * r:E * r + E], wq_t[h]).then_inc(wq_in, 16)
                for g in range(1, G):
                    sp.dma_start(x_in[:, GT * g:GT * g + GT, :], x_v[:, GT * g:GT * g + GT, :]).then_inc(x_loaded, 16)
                sp.dma_start(w1_int, fc1_q.rearrange("(k p) f -> p k f", p=P)).then_inc(weights_in, 16)
                sp.dma_start(w2_int, fc2_q.rearrange("(k p) f -> p k f", p=P)).then_inc(weights_in, 16)
                sp.dma_start(wp[:, :, :], wp_t.rearrange("(k p) f -> p k f", p=P)).then_inc(weights_in, 16)
                sp.dma_start(w1_scale, fc1_s.partition_broadcast(P)).then_inc(weights_in, 16)
                sp.dma_start(w2_scale, fc2_s.partition_broadcast(P)).then_inc(weights_in, 16)
                sp.dma_start(bp_ga[:, :], bp.partition_broadcast(P)).then_inc(weights_in, 16)
                sp.dma_start(b2_gb[:, :], fc2_b.partition_broadcast(P)).then_inc(weights_in, 16)
                sp.dma_start(gamma_col[:, :], gamma).then_inc(weights_in, 16)
                sp.dma_start(beta_col[:, :], beta).then_inc(weights_in, 16)
                sp.dma_start(b1_col[:, :], fc1_b).then_inc(weights_in, 16)
                def store_parts(g):
                    sp.wait_ge(part_c, g + 1)
                    for k in range(DC):
                        sp.dma_start(parts_dram[:, k * P:(k + 1) * P, bass.ds(g * BANK, BANK)].rearrange("s p n -> p s n"),
                                     q_parts[:, :, k, :]).then_inc(parts_stored, 16)

                rounds(sp, store_parts, G)
                sp.wait_ge(parts_stored, 16 * DC * G)
                sp.wait_ge(weights_in, 160)

            @block.gpsimd
            def _(pool):
                pool.wait_ge(const_in, 16)
                pool.memset(wq_diag, 0.0).then_inc(diag_zero, 1)
                pool.memset(ones, 1.0).then_inc(c_step, 1)
                def small_parts(g):
                    pool.wait_ge(rest_ab, g + 1)
                    carry(pool)
                    pool.tensor_copy(q_parts[:, 1, :, :], q_rest).then_inc(part_b, 1)
                    pool.wait_ge(part_b, g + 1)
                    pool.tensor_tensor(q_parts[:, 2, :, :], q_rest, q_parts[:, 1, :, :], ALU.subtract).then_inc(part_c, 1)
                    pool.wait_ge(v_copied, g + 1)
                    wait(pool, norms_ready, g)
                    v_now = values[:, bass.ds(g * GT, GT), :]
                    pool.tensor_tensor(q_sq.rearrange("p (t d) -> p t d", t=GT), v_now, v_now, ALU.mult).then_inc(sq_ready, 1)

                rounds(pool, small_parts, G)
            @block.scalar
            def _(act):
                act.wait_ge(c_loaded, 16)
                act.activation(silu_c[:, 1, :], silu_c[:, 0, :], ACT.Exp, scale=-1.0).then_inc(c_exp, 1)
                for i in range(3):
                    act.wait_ge(mod_mm, i + 1)
                    act.activation(mod[:, 2 * i:2 * i + 2, :], ps_mod.rearrange("p (s d) -> p s d", s=2), ACT.Copy).then_inc(mod_copied, 1)
                act.wait_ge(col_ready, 2)
                def evacuate(g):
                    act.wait_ge(z_turned, g + 1)
                    wait(act, q_tok_mm, g)
                    for k in range(DC):
                        last = act.activation(h_feat[:, k, :], ps_turn[:, k, :], ACT.Identity,
                                              bias=mod_col[:, k:k + 1], scale=mod_col[:, 2 + k:3 + k])
                    last.then_inc(h_ready, 1)
                    act.wait_ge(q_feat_mm, g + 1)
                    wait(act, parts_stored, g * (16 * DC))
                    act.activation(q_parts[:, 0, :, :], ps_qf, ACT.Copy, scale=2.0).then_inc(part_a, 1)
                    act.wait_ge(q_tok_mm, g + 1)
                    act.activation(values[:, bass.ds(g * GT, GT), :],
                                   ps_qt.rearrange("p b (t d) -> p (b t) d", d=D), ACT.Copy).then_inc(v_copied, 1)

                rounds(act, evacuate, G)
            @block.tensor
            def _(pe):
                pe.wait_ge(wide_ready, 1)
                pe.wait_ge(wmod_in, 16)
                for i in range(3):
                    if i:
                        pe.wait_ge(mod_copied, i)
                    for k in range(DC):
                        last = pe.matmul(ps_mod, silu_wide[:, k, :], wmod_sb[:, k, i * BANK:(i + 1) * BANK],
                                         start=(k == 0), stop=(k == DC - 1))
                    last.then_inc(mod_mm, 1)
                for j in range(4):
                    for k in range(DC):
                        last = pe.matmul(ps_col[:, j:j + 1], wmod_sb[:, k, j * P:(j + 1) * P], silu_c[:, 3, k:k + 1],
                                         start=(k == 0), stop=(k == DC - 1))
                last.then_inc(col_mm, 1)
                pe.wait_ge(const_in, 16)
                pe.wait_ge(wq_in, 16 * H)
                def queries(g):
                    pe.wait_ge(z_ready, g + 1)
                    wait(pe, h_ready, g)
                    for k in range(DC):
                        for t in range(GT):
                            last = pe.transpose(ps_turn[:, k, t * P:(t + 1) * P], z_tok[:, t, k * P:(k + 1) * P], ident[:, :])
                    last.then_inc(z_turned, 1)
                    pe.wait_ge(h_ready, g + 1)
                    wait(pe, rest_ab, g)
                    for k in range(DC):
                        last = pe.matmul(ps_qf[:, k, :], wq_diag[:, k, :], h_feat[:, k, :], start=True, stop=True)
                    last.then_inc(q_feat_mm, 1)
                    wait(pe, v_copied, g)
                    for t in range(GT):
                        for k in range(DC):
                            col = (t % 2) * D + k * P
                            last = pe.matmul(ps_qt[:, t // 2, col:col + P], h_feat[:, k, t * P:(t + 1) * P], wq_diag[:, k, :],
                                             start=True, stop=True)
                    last.then_inc(q_tok_mm, 1)

                rounds(pe, queries, G)
            @block.vector
            def _(dve):
                dve.wait_ge(c_exp, 1)
                dve.tensor_scalar(silu_c[:, 2, :], silu_c[:, 1, :], 1.0, None, ALU.add).then_inc(c_step, 1)
                dve.wait_ge(c_step, 2)
                dve.reciprocal(silu_c[:, 1, :], silu_c[:, 2, :]).then_inc(c_step, 1)
                dve.wait_ge(c_step, 3)
                dve.tensor_tensor(silu_c[:, 3, :], silu_c[:, 0, :], silu_c[:, 1, :], ALU.mult).then_inc(c_step, 1)
                dve.wait_ge(c_step, 4)
                for k in range(DC):
                    last = dve.tensor_scalar(silu_wide[:, k, :], ones, silu_c[:, 3, k:k + 1], None, ALU.mult)
                last.then_inc(wide_ready, 1)

                def normalise(g):
                    for t in range(GT):
                        last = dve.bn_stats(stats[:, t, :], x_in[:, bass.ds(g * GT + t, 1), :].rearrange("p a d -> p (a d)"))
                    last.then_inc(stats_done, 1)
                    dve.wait_ge(stats_done, g + 1)
                    dve.memset(carrier, 0.0)
                    for t in range(GT):
                        last = dve.bn_aggr(moments[:, t, :], stats[:, t, :])
                    last.then_inc(moments_done, 1)
                    dve.wait_ge(moments_done, g + 1)
                    rsqrt(dve, rstd, moments[:, :, 1], rsqrt_work, rstd_done, g)
                    wait(dve, z_turned, g)
                    for t in range(GT):
                        last = dve.tensor_scalar(z_tok[:, t, :], x_in[:, bass.ds(g * GT + t, 1), :].rearrange("p a d -> p (a d)"),
                                                 moments[:, t, 0:1], rstd[:, t:t + 1], ALU.subtract, ALU.mult)
                    last.then_inc(z_ready, 1)

                def split_and_norms(g):
                    dve.wait_ge(part_a, g + 1)
                    wait(dve, part_c, g)
                    dve.scalar_tensor_tensor(out=q_rest, in0=ps_qf, scalar=2.0, in1=q_parts[:, 0, :, :],
                                             op0=ALU.mult, op1=ALU.subtract).then_inc(rest_ab, 1)
                    dve.wait_ge(sq_ready, g + 1)
                    dve.tensor_reduce(norms[:, bass.ds(g * GT, GT), :], q_sq.rearrange("p (t h e) -> p t h e", t=GT, h=H),
                                      AX.X, ALU.add).then_inc(norms_ready, 1)

                dve.wait_ge(x0_loaded, 16)
                normalise(0)
                dve.wait_ge(col_mm, 1)
                dve.tensor_copy(mod_col[:, 0:2], ps_col[:, 0:2]).then_inc(col_ready, 1)
                dve.tensor_scalar(mod_col[:, 2:4], ps_col[:, 2:4], 1.0, None, ALU.add).then_inc(col_ready, 1)
                dve.wait_ge(x_loaded, 16 * (G - 1))
                def both(g):
                    normalise(g + 1)
                    split_and_norms(g)

                rounds(dve, both, G - 1)
                split_and_norms(G - 1)

                dve.wait_ge(mod_copied, 3)
                gates = mod[:, 2:6:3, :]
                dve.tensor_scalar(sign, gates, 0.0, 2.0, ALU.is_ge, ALU.mult).then_inc(mod_step, 1)
                dve.tensor_scalar(negated, gates, -1.0, None, ALU.mult).then_inc(mod_step, 1)
                dve.wait_ge(mod_step, 2)
                dve.tensor_scalar(sign, sign, -1.0, None, ALU.add).then_inc(mod_step, 1)
                dve.tensor_tensor(negated, negated, gates, ALU.max).then_inc(mod_step, 1)
                dve.wait_ge(mod_step, 4)
                dve.scalar_tensor_tensor(out=gates, in0=negated, scalar=0.25, in1=sign, op0=ALU.max, op1=ALU.mult).then_inc(mod_step, 1)
                dve.tensor_scalar(mod[:, 4, :], mod[:, 4, :], 1.0, None, ALU.add).then_inc(mod_step, 1)
                dve.wait_ge(mod_step, 6)
                dve.tensor_scalar(sign[:, 0, :], mod[:, 5, :], 0.5, None, ALU.mult).then_inc(mod_step, 1)
                dve.wait_ge(mod_step, 7)
                dve.wait_ge(weights_in, 160)
                dve.tensor_tensor(bp_ga[:, :], bp_ga[:, :], mod[:, 2, :], ALU.mult).then_inc(w_step, 1)
                dve.tensor_tensor(b2_gb[:, :], b2_gb[:, :], sign[:, 0, :], ALU.mult).then_inc(w_step, 1)
                for k in range(DC):
                    dve.tensor_tensor(wp[:, k, :], wp[:, k, :], mod[:, 2, :], ALU.mult).then_inc(w_step, 1)
                dve.scalar_tensor_tensor(out=w1[:, :, :], in0=w1_int, scalar=-128.0, in1=w1_scale,
                                         op0=ALU.add, op1=ALU.mult).then_inc(w_step, 1)
                dve.scalar_tensor_tensor(out=w2[:, :, :], in0=w2_int, scalar=-128.0, in1=w2_scale,
                                         op0=ALU.add, op1=ALU.mult).then_inc(w_step, 1)
                dve.wait_ge(w_step, 6)
                for k in range(FT):
                    dve.tensor_tensor(w2[:, k, :], w2[:, k, :], sign[:, 0, :], ALU.mult).then_inc(w_step, 1)
                dve.wait_ge(w_step, 6 + FT)

        a.close()
        stacks = Scope(ctx, nc, "stacks")
        stack_k = stacks.take("stack_k", N).bitcast(BF16).rearrange("p (b n) -> p b n", b=2)
        stack_q = stacks.take("stack_q", N).bitcast(BF16).rearrange("p (b n) -> p b n", b=2)
        a = Scope(ctx, nc, "shift")
        top_by_head = a.take("top_by_head", 1)
        top_diag = a.take("top_diag", H)
        top_wide = a.take("top_wide", H)
        ones16 = a.take("ones16", P)
        peak = a.take("peak", 1)
        fits = a.take("fits", 1).bitcast(I32)
        half_max = a.take("half_max", 2 * TILES).rearrange("p (t s) -> p t s", t=TILES)
        shift_now = a.take("shift_now", TILES * H)
        shift_rest = a.take("shift_rest", BANK)
        shift_parts = a.take("shift_parts", 3 * BANK // 2).bitcast(BF16).rearrange("p (s n) -> p s n", s=3)

        top_step, top_turned, top_bc, guess_step, fits_ready = (sem(n) for n in (
            "top_step", "top_turned", "top_bc", "guess_step", "fits_ready"))
        root_done = sem("root_done")
        max_stacks, row_scores, head_max = sem("max_stacks"), sem("row_scores"), sem("head_max")
        half_free = [sem("half_free0"), sem("half_free1")]
        shift_set, shift_turned, split_step, shift_stored = (sem(n) for n in (
            "shift_set", "shift_turned", "split_step", "shift_stored"))

        def load_stacks(eng, head, slot, done, with_shift):
            rows = bass.ds(head * E, E)

            def put(stack, first, count, src):
                eng.dma_start(stack[first:first + count, bass.ds(slot, 1), :].rearrange("p a n -> p (a n)"), src).then_inc(done, 16)

            for block_row, part in enumerate((0, 0, 0, 1, 1, 2)):
                put(stack_k, block_row * E, E, parts_dram[part, rows, :])
            for block_row, part in enumerate((0, 1, 2, 0, 1, 0)):
                put(stack_q, block_row * E, E, parts_dram[part, rows, :])
            if with_shift:
                for part in range(3):
                    put(stack_q, ROWS + part, 1, shift_dram[part, bass.ds(head, 1), :])

        ps_half = [a.banks("half0", 4), a.banks("half1", 4)]
        turned = ps_half[0][:, 0, :]
        FILL, FILL_SHIFT = 16 * 12, 16 * 15

        with nc.Block() as block:

            @block.sync
            def _(sp):
                sp.wait_ge(fits_ready, 1)
                with sp.If(sp.value_load(fits[0:1, 0:1], min_val=0, max_val=1) == 0):
                    load_stacks(sp, 0, 0, max_stacks, False)
                    sp.wait_ge(max_stacks, FILL)
                    load_stacks(sp, 1, 1, max_stacks, False)
                    with sp.Fori(2, H) as h:
                        sp.wait_ge(row_scores, (h - 1) * (2 * TILES) + 1)
                        load_stacks(sp, h, h % 2, max_stacks, False)
                    sp.wait_ge(max_stacks, FILL * H)
                sp.wait_ge(split_step, 5)
                dst = shift_dram.rearrange("s h (o t n) -> t s h o n", t=TILES // 4, n=P)
                for t in range(TILES // 4):
                    for part in range(3):
                        sp.dma_start(dst[t, part], shift_parts[H * t:H * (t + 1), part, :].rearrange("h (o n) -> h o n", o=4))\
                          .then_inc(shift_stored, 16)
                sp.wait_ge(shift_stored, 16 * 3 * TILES // 4)

            @block.tensor
            def _(pe):
                pe.wait_ge(top_step, 2)
                pe.transpose(turned[0:H, 0:P], top_wide, ident[:, :]).then_inc(top_turned, 1)
                pe.wait_ge(top_step, 4)
                pe.matmul(ps_half[0][:, 1, 0:H], ones16[0:H, :], top_diag[0:H, :], start=True, stop=True).then_inc(top_bc, 1)
                pe.wait_ge(fits_ready, 1)
                with pe.If(pe.value_load(fits[0:1, 0:1], min_val=0, max_val=1) == 0):
                    with pe.Fori(0, H) as h:
                        with pe.Fori(0, TILES) as t:
                            pe.wait_ge(max_stacks, (h + 1) * FILL)
                            for half in range(2):
                                pe.wait_ge(half_free[half], h * TILES + (t + 1))
                                for j in range(4 * half, 4 * half + 4):
                                    last = pe.matmul(ps_half[half][:, j % 4, :],
                                                     stack_k[0:ROWS, bass.ds(h % 2, 1), bass.ds(t * P, P)].rearrange("p a n -> p (a n)"),
                                                     stack_q[0:ROWS, bass.ds(h % 2, 1), j * BANK:(j + 1) * BANK].rearrange("p a n -> p (a n)"),
                                                     start=True, stop=True)
                                last.then_inc(row_scores, 1)
                pe.wait_ge(shift_set, 1)
                for o in range(4):
                    last = pe.transpose(turned[:, o * P:(o + 1) * P], shift_now[:, o * P:(o + 1) * P], ident[:, :])
                last.then_inc(shift_turned, 1)

            @block.gpsimd
            def _(pool):
                pool.memset(ones16, 1.0).then_inc(top_step, 1)

            @block.scalar
            def _(act):
                act.wait_ge(guess_step, 1)
                act.activation(shifts[:, :, :], shifts[:, :, :], ACT.Sqrt, scale=4.0).then_inc(root_done, 1)

            @block.vector
            def _(dve):
                dve.wait_ge(top_step, 1)
                dve.tensor_reduce(top_wide, norms[:, :, :].rearrange("p t h -> p h t"), AX.X, ALU.max).then_inc(top_step, 1)
                dve.wait_ge(top_turned, 1)
                dve.tensor_reduce(top_by_head[0:H, :], turned[0:H, 0:P], AX.X, ALU.max).then_inc(top_step, 1)
                dve.wait_ge(top_step, 3)
                dve.tensor_scalar(top_diag[0:H, :], ident[0:H, 0:H], top_by_head[0:H, 0:1], None, ALU.mult).then_inc(top_step, 1)
                dve.wait_ge(top_bc, 1)
                dve.tensor_copy(top_wide, ps_half[0][:, 1, 0:H]).then_inc(top_step, 1)
                dve.wait_ge(top_step, 5)
                dve.tensor_tensor(shifts[:, :, :], norms[:, :, :], top_wide.unsqueeze(1).broadcast_to([P, TILES, H]), ALU.mult).then_inc(guess_step, 1)
                dve.tensor_reduce(peak, top_wide, AX.X, ALU.max).then_inc(top_step, 1)
                dve.wait_ge(top_step, 6)
                dve.tensor_scalar(fits, peak, REACH, None, ALU.is_le).then_inc(fits_ready, 1)
                dve.wait_ge(root_done, 1)
                dve.scalar_tensor_tensor(out=shifts[:, :, :], in0=norms[:, :, :], scalar=2.0, in1=shifts[:, :, :],
                                         op0=ALU.mult, op1=ALU.add).then_inc(guess_step, 1)
                dve.wait_ge(guess_step, 2)
                dve.wait_ge(fits_ready, 1)
                with dve.If(dve.value_load(fits[0:1, 0:1], min_val=0, max_val=1) == 0):
                    for half in range(2):
                        dve.memset(half_max[:, :, half:half + 1], 0.0).then_inc(half_free[half], 1)
                    with dve.Fori(0, H) as h:
                        with dve.Fori(0, TILES) as t:
                            for half in range(2):
                                dve.wait_ge(row_scores, h * (2 * TILES) + t * 2 + (half + 1))
                                dve.tensor_reduce(half_max[:, bass.ds(t, 1), half:half + 1], ps_half[half],
                                                  AX.XY, ALU.max).then_inc(half_free[half], 1)
                        for half in range(2):
                            dve.wait_ge(half_free[half], h * TILES + (TILES + 1))
                        dve.tensor_reduce(shifts[:, :, bass.ds(h, 1)], half_max, AX.X, ALU.max).then_inc(head_max, 1)
                        dve.wait_ge(head_max, h + 1)
                dve.tensor_copy(shift_now, shifts[:, :, :].rearrange("p t h -> p (t h)")).then_inc(shift_set, 1)
                dve.wait_ge(shift_turned, 1)
                dve.tensor_copy(shift_parts[:, 0, :], turned).then_inc(split_step, 1)
                dve.wait_ge(split_step, 1)
                dve.tensor_tensor(shift_rest, turned, shift_parts[:, 0, :], ALU.subtract).then_inc(split_step, 1)
                dve.wait_ge(split_step, 2)
                dve.tensor_copy(shift_parts[:, 1, :], shift_rest).then_inc(split_step, 1)
                dve.wait_ge(split_step, 3)
                dve.tensor_tensor(shift_rest, shift_rest, shift_parts[:, 1, :], ALU.subtract).then_inc(split_step, 1)
                dve.wait_ge(split_step, 4)
                dve.tensor_copy(shift_parts[:, 2, :], shift_rest).then_inc(split_step, 1)

        a.close()
        a = Scope(ctx, nc, "attend")
        probs = [a.take(f"probs{i}", 2 * BANK).rearrange("p (b n) -> p b n", b=2) for i in range(P_RING)]
        v_now = [a.take(f"v_now{i}", TILES * 32).rearrange("p (t e) -> p t e", t=TILES) for i in range(3)]
        sums_sb = a.take("sums_sb", BANK)
        inverse = a.take("inverse", GT)
        whole = a.take("whole", GT * (E + 1)).rearrange("p (t e) -> p t e", t=GT)
        quarters_added = sem("quarters_added")

        minus_set, v_filled, stacks_in = sem("minus_set"), sem("v_filled"), sem("stacks_in")
        scores_ready, exps_done, units_done = sem("scores_ready"), sem("exps_done"), sem("units_done")
        v_ready, sums_copied, sums_turned, inverse_ready, chunk_done = (sem(n) for n in (
            "v_ready", "sums_copied", "sums_turned", "inverse_ready", "chunk_done"))
        ps_scores = [a.banks(f"scores{i}", 2) for i in range(S_RING)]
        ps_sums, ps_turned = a.banks("sums", 1)[:, 0, :], a.banks("turned", 1)[:, 0, :]

        def chunks(eng, body):
            body(0, 0)
            with eng.Fori(0, (NCH - 2) // 3) as b:
                for r in range(3):
                    body(b * 3 + (r + 1), (r + 1) % 3)
            body(NCH - 1, (NCH - 1) % 3)

        with nc.Block() as block:

            @block.sync
            def _(sp):
                load_stacks(sp, 0, 0, stacks_in, True)
                sp.wait_ge(stacks_in, FILL_SHIFT)
                load_stacks(sp, 1, 1, stacks_in, True)
                with sp.Fori(2, H) as h:
                    sp.wait_ge(scores_ready, (h - 1) * (G * PAIRS) + 1)
                    load_stacks(sp, h, h % 2, stacks_in, True)
                sp.wait_ge(stacks_in, FILL_SHIFT * H)

            @block.gpsimd
            def _(pool):
                pool.memset(stack_k[ROWS:STACK, :, :], -1.0).then_inc(minus_set, 1)
                pool.wait_ge(minus_set, 1)
                for i in range(3):
                    pool.memset(v_now[i], 0.0).then_inc(v_filled, 1)
                    pool.wait_ge(v_filled, 2 * i + 1)
                    pool.memset(v_now[i][:, :, E:E + 1], 1.0).then_inc(v_filled, 1)
                    pool.wait_ge(v_filled, 2 * i + 2)

                def copy_values(c, r):
                    if not isinstance(c, int) or c >= 3:
                        pool.wait_ge(v_ready, c)
                        pool.wait_ge(units_done, c * UNITS - 2 * UNITS)
                        carry(pool)
                    pool.tensor_copy(v_now[r][:, :, 0:E], values[:, :, bass.ds((c // G) * E, E)]).then_inc(v_ready, 1)

                copy_values(0, 0)
                copy_values(1, 1)
                copy_values(2, 2)
                with pool.Fori(1, (NCH - 2) // 3) as b:
                    for r in range(3):
                        copy_values(b * 3 + r, r)
                copy_values(NCH - 2, (NCH - 2) % 3)
                copy_values(NCH - 1, (NCH - 1) % 3)

            @block.scalar
            def _(act):
                def exps(c, r):
                    for k in range(PAIRS):
                        act.wait_ge(scores_ready, c * PAIRS + (k + 1))
                        slot = k % P_RING
                        if k % 2 == 0 and (not isinstance(c, int) or c or k >= P_RING):
                            act.wait_ge(units_done, c * UNITS + (k - P_RING) // 2 + 1)
                        act.activation(probs[slot], ps_scores[(r + k) % S_RING], ACT.Exp).then_inc(exps_done, 1)
                chunks(act, exps)

            @block.tensor
            def _(pe):
                pe.wait_ge(minus_set, 1)
                pe.wait_ge(v_filled, 6)

                def scores(c, r, k):
                    if not isinstance(c, int) or c or k >= S_RING:
                        pe.wait_ge(exps_done, c * PAIRS + (k - S_RING + 1))
                    slot = bass.ds((c // G) % 2, 1)
                    for b in range(2):
                        t = 2 * k + b
                        last = pe.matmul(ps_scores[(r + k) % S_RING][:, b, :],
                                         stack_k[0:STACK, slot, t * P:(t + 1) * P].rearrange("p a n -> p (a n)"),
                                         stack_q[0:STACK, slot, bass.ds((c % G) * BANK, BANK)].rearrange("p a n -> p (a n)"),
                                         start=True, stop=True)
                    last.then_inc(scores_ready, 1)

                def weigh(c, r, u):
                    if u == 0:
                        pe.wait_ge(v_ready, c + 1)
                        if not isinstance(c, int) or c:
                            pe.wait_ge(sums_copied, c)
                    pe.wait_ge(exps_done, c * PAIRS + (2 * u + 2))
                    for q in range(4):
                        t = 4 * u + q
                        slot = (t // 2) % P_RING
                        last = pe.matmul(ps_sums[32 * q:32 * q + 32, :], v_now[r][:, t, :], probs[slot][:, t % 2, :],
                                         start=(u == 0), stop=(u == UNITS - 1))
                    last.then_inc(units_done, 1)

                def turn_sums(c):
                    pe.wait_ge(sums_copied, c + 1)
                    if not isinstance(c, int) or c:
                        pe.wait_ge(quarters_added, c)
                    for t in range(GT):
                        last = pe.transpose(ps_turned[:, t * P:(t + 1) * P], sums_sb[:, t * P:(t + 1) * P], ident[:, :])
                    last.then_inc(sums_turned, 1)

                def chunk(c, r):
                    head_start = c // G
                    pe.wait_ge(stacks_in, (head_start + 1) * FILL_SHIFT)
                    before = c - 1
                    for u in range(UNITS):
                        scores(c, r, 2 * u)
                        scores(c, r, 2 * u + 1)
                        if u >= LAG:
                            weigh(c, r, u - LAG)
                        elif not isinstance(c, int) or c:
                            weigh(before, (r - 1) % 3, u - LAG + UNITS)
                        if u == LAG + 1 and (not isinstance(c, int) or c):
                            turn_sums(before)

                chunks(pe, chunk)
                for u in range(UNITS - LAG, UNITS):
                    weigh(NCH - 1, (NCH - 1) % 3, u)
                turn_sums(NCH - 1)

            @block.vector
            def _(dve):
                def copy_sums(c):
                    dve.wait_ge(units_done, c * UNITS + UNITS)
                    if not isinstance(c, int) or c:
                        dve.wait_ge(sums_turned, c)
                    dve.tensor_copy(sums_sb, ps_sums).then_inc(sums_copied, 1)

                def divide(c):
                    dve.wait_ge(sums_turned, c + 1)
                    dve.tensor_reduce(whole, ps_turned.rearrange("p (t q e) -> p t e q", t=GT, q=4)[:, :, 0:E + 1, :],
                                      AX.X, ALU.add).then_inc(quarters_added, 1)
                    dve.wait_ge(quarters_added, c + 1)
                    dve.reciprocal(inverse, whole[:, :, E]).then_inc(inverse_ready, 1)
                    dve.wait_ge(inverse_ready, c + 1)
                    dve.tensor_tensor(att[:, bass.ds((c % G) * GT, GT), bass.ds((c // G) * E, E)], whole[:, :, 0:E],
                                      inverse.unsqueeze(2).broadcast_to([P, GT, E]), ALU.mult).then_inc(chunk_done, 1)

                copy_sums(0)
                with dve.Fori(1, NCH) as c:
                    divide(c - 1)
                    copy_sums(c)
                divide(NCH - 1)
                dve.wait_ge(chunk_done, NCH)

        a.close()
        stacks.close()
        a = Scope(ctx, nc, "out")

        def tok(name):
            return a.take(name, GT * D).rearrange("p (t d) -> p t d", t=GT)

        x_res = a.take("x_res", TILES * D).rearrange("p (t d) -> p t d", d=D)
        att_now, x1, z1, hid, mix = tok("att_now"), tok("x1"), tok("z1"), tok("hid"), tok("mix")
        att_feat = a.take("att_feat", DC * BANK).rearrange("p (k n) -> p k n", k=DC)
        base = [tok("base0"), tok("base1")]
        y_out = [tok("y_out0"), tok("y_out1")]
        ps_turn, ps_proj, ps_down = a.banks("turn", 2), a.banks("proj", 2), a.banks("down", 2)
        ps_up = [a.banks("up0", 1)[:, 0, :], a.banks("up1", 1)[:, 0, :]]
        ffn_in = a.take("ffn_in", DC * BANK).rearrange("p (k n) -> p k n", k=DC)
        hidden = a.take("hidden", FT * BANK).rearrange("p (k n) -> p k n", k=FT)
        st2 = a.take("st2", GT * 6).rearrange("p (t s) -> p t s", t=GT)
        mo2 = a.take("mo2", 2 * GT * 2).rearrange("p (r t s) -> p r t s", r=2, t=GT)
        rs2 = a.take("rs2", 2 * GT).rearrange("p (r t) -> p r t", r=2)
        carrier2 = a.take("carrier2", 1)
        rsqrt_work2 = a.take("rsqrt_work2", 3 * GT).rearrange("p (s t) -> p s t", s=3)

        names = ("xr_in", "att_copied", "att_turned", "af_ready", "proj_mm", "x1_ready", "xb_ready", "n_stats", "n_mom", "n_rstd",
                 "z1_ready", "scaled", "hid_ready", "mix_ready", "base_ready", "z2_ready", "z2_turned", "fi_ready",
                 "up_mm", "act_done", "down_mm", "y_ready")
        (xr_in, att_copied, att_turned, af_ready, proj_mm, x1_ready, xb_ready, n_stats, n_mom, n_rstd,
         z1_ready, scaled, hid_ready, mix_ready, base_ready, z2_ready, z2_turned, fi_ready,
         up_mm, act_done, down_mm, y_ready) = (sem(n) for n in names)
        y_stored = [sem("y_stored0"), sem("y_stored1")]
        z2 = z1

        def wide(v):
            return v.unsqueeze(1).broadcast_to([P, GT, D])

        with nc.Block() as block:

            @block.sync
            def _(sp):
                for g in range(G):
                    sp.dma_start(x_res[:, GT * g:GT * g + GT, :], x_v[:, GT * g:GT * g + GT, :]).then_inc(xr_in, 16)
                def store(b):
                    for r in range(2):
                        g = b * 2 + r
                        sp.wait_ge(y_ready, g + 1)
                        sp.dma_start(out_v[:, bass.ds(g * GT, GT), :], y_out[r]).then_inc(y_stored[r], 16)

                rounds(sp, store, G // 2)
                for r in range(2):
                    sp.wait_ge(y_stored[r], 16 * (G // 2))

            @block.gpsimd
            def _(pool):
                pool.wait_ge(xr_in, 16 * G)
                def pair(b):
                    for r in range(2):
                        g = b * 2 + r
                        wait(pool, att_turned, g)
                        carry(pool)
                        pool.tensor_copy(att_now, att[:, bass.ds(g * GT, GT), :]).then_inc(att_copied, 1)
                        xr = x_res[:, bass.ds(g * GT, GT), :]
                        pool.tensor_tensor(xr, xr, wide(bp_ga[:, :]), ALU.add).then_inc(xb_ready, 1)
                        pool.wait_ge(scaled, g + 1)
                        pool.tensor_tensor(hid, hid, wide(mod[:, 3, :]), ALU.add).then_inc(hid_ready, 1)
                        pool.wait_ge(hid_ready, g + 1)
                        pool.tensor_tensor(mix, hid, wide(mod[:, 5, :]), ALU.mult).then_inc(mix_ready, 1)
                        pool.wait_ge(mix_ready, g * 3 + 1)
                        pool.tensor_tensor(mix, mix, wide(b2_gb[:, :]), ALU.add).then_inc(mix_ready, 1)
                        pool.wait_ge(mix_ready, g * 3 + 2)
                        wait(pool, y_ready, b * 2)
                        pool.tensor_tensor(base[r], mix, x1, ALU.add).then_inc(mix_ready, 1)

                rounds(pool, pair, G // 2)
            @block.scalar
            def _(act):
                def turn_att(g):
                    act.wait_ge(att_turned, g + 1)
                    wait(act, proj_mm, g)
                    act.activation(att_feat, ps_turn, ACT.Copy).then_inc(af_ready, 1)

                def turn_z2(g):
                    act.wait_ge(z2_turned, g + 1)
                    wait(act, up_mm, g * FT)
                    for k in range(DC):
                        last = act.activation(ffn_in[:, k, :], ps_turn[:, k, :], ACT.Identity,
                                              bias=beta_col[:, k:k + 1], scale=gamma_col[:, k:k + 1])
                    last.then_inc(fi_ready, 1)

                def silus(g):
                    for f in range(FT):
                        act.wait_ge(up_mm, g * FT + (f + 1))
                        if f == 0:
                            wait(act, down_mm, g)
                        act.activation(hidden[:, f, :], ps_up[f % 2], ACT.Silu, bias=b1_col[:, f:f + 1])\
                           .then_inc(act_done, 1)

                turn_att(0)
                turn_z2(0)
                def step(g):
                    turn_att(g + 1)
                    silus(g)
                    turn_z2(g + 1)

                rounds(act, step, G - 1)
                silus(G - 1)

            @block.tensor
            def _(pe):
                def project(g):
                    pe.wait_ge(att_copied, g + 1)
                    wait(pe, fi_ready, g)
                    for k in range(DC):
                        for t in range(GT):
                            last = pe.transpose(ps_turn[:, k, t * P:(t + 1) * P], att_now[:, t, k * P:(k + 1) * P], ident[:, :])
                    last.then_inc(att_turned, 1)
                    pe.wait_ge(af_ready, g + 1)
                    wait(pe, x1_ready, g)
                    for t in range(GT):
                        for k in range(DC):
                            last = pe.matmul(ps_proj[:, t // 2, (t % 2) * D:(t % 2 + 1) * D], att_feat[:, k, t * P:(t + 1) * P],
                                             wp[:, k, :], start=(k == 0), stop=(k == DC - 1))
                    last.then_inc(proj_mm, 1)

                def turn(g):
                    pe.wait_ge(z2_ready, g + 1)
                    pe.wait_ge(af_ready, g + 1)
                    for k in range(DC):
                        for t in range(GT):
                            last = pe.transpose(ps_turn[:, k, t * P:(t + 1) * P], z2[:, t, k * P:(k + 1) * P], ident[:, :])
                    last.then_inc(z2_turned, 1)

                def up(g):
                    pe.wait_ge(fi_ready, g + 1)
                    for f in range(FT):
                        wait(pe, act_done, g * FT + max(f - 1, 0))
                        for k in range(DC):
                            last = pe.matmul(ps_up[f % 2], w1[:, k, f * P:(f + 1) * P], ffn_in[:, k, :],
                                             start=(k == 0), stop=(k == DC - 1))
                        last.then_inc(up_mm, 1)

                def down(g):
                    pe.wait_ge(act_done, g * FT + FT)
                    wait(pe, y_ready, g)
                    for t in range(GT):
                        for f in range(FT):
                            last = pe.matmul(ps_down[:, t // 2, (t % 2) * D:(t % 2 + 1) * D], hidden[:, f, t * P:(t + 1) * P],
                                             w2[:, f, :], start=(f == 0), stop=(f == FT - 1))
                    last.then_inc(down_mm, 1)

                project(0)
                turn(0)
                def step(g):
                    project(g + 1)
                    up(g)
                    turn(g + 1)
                    down(g)

                rounds(pe, step, G - 1)
                up(G - 1)
                down(G - 1)

            @block.vector
            def _(dve):
                def stats_of(src, r, n):
                    for t in range(GT):
                        last = dve.bn_stats(st2[:, t, :], src[:, t, :])
                    last.then_inc(n_stats, 1)
                    dve.wait_ge(n_stats, n + 1)
                    dve.memset(carrier2, 0.0)
                    for t in range(GT):
                        last = dve.bn_aggr(mo2[:, r, t, :], st2[:, t, :])
                    last.then_inc(n_mom, 1)
                    dve.wait_ge(n_mom, n + 1)
                    rsqrt(dve, rs2[:, r, :], mo2[:, r, :, 1], rsqrt_work2, n_rstd, n)

                def middle(g):
                    dve.wait_ge(proj_mm, g + 1)
                    dve.wait_ge(xb_ready, g + 1)
                    wait(dve, mix_ready, g * 3)
                    dve.tensor_tensor(x1, ps_proj.rearrange("p b (t d) -> p (b t) d", d=D), x_res[:, bass.ds(g * GT, GT), :],
                                      ALU.add).then_inc(x1_ready, 1)
                    dve.wait_ge(x1_ready, g + 1)
                    wait(dve, z2_turned, g)
                    stats_of(x1, 0, g * 2)
                    for t in range(GT):
                        last = dve.tensor_scalar(z1[:, t, :], x1[:, t, :], mo2[:, 0, t, 0:1], rs2[:, 0, t:t + 1], ALU.subtract, ALU.mult)
                    last.then_inc(z1_ready, 1)
                    dve.wait_ge(z1_ready, g + 1)
                    dve.tensor_tensor(hid, z1, wide(mod[:, 4, :]), ALU.mult).then_inc(scaled, 1)
                    dve.wait_ge(hid_ready, g + 1)
                    stats_of(hid, 1, g * 2 + 1)
                    dve.wait_ge(scaled, g + 1)
                    for t in range(GT):
                        last = dve.tensor_scalar(z2[:, t, :], hid[:, t, :], mo2[:, 1, t, 0:1], rs2[:, 1, t:t + 1], ALU.subtract, ALU.mult)
                    last.then_inc(z2_ready, 1)

                def finish(g, r, b):
                    dve.wait_ge(down_mm, g + 1)
                    dve.wait_ge(mix_ready, g * 3 + 3)
                    wait(dve, y_stored[r], b * 16)
                    dve.tensor_tensor(y_out[r], ps_down.rearrange("p b (t d) -> p (b t) d", d=D), base[r], ALU.add)\
                       .then_inc(y_ready, 1)

                middle(0)
                def pair(b):
                    for r in range(2):
                        middle(b * 2 + (r + 1))
                        finish(b * 2 + r, r, b)

                rounds(dve, pair, G // 2 - 1)
                middle(G - 1)
                finish(G - 2, 0, G // 2 - 1)
                finish(G - 1, 1, G // 2 - 1)


_INS = ['L0_attn_x', 'L0_attn_Wq', 'L0_attn_Wp', 'L0_attn_bp', 'L0_ffn_ln_gamma', 'L0_ffn_ln_beta', 'L0_ffn_fc1_q',
        'L0_ffn_fc1_scales', 'L0_ffn_fc1_bias', 'L0_ffn_fc2_q', 'L0_ffn_fc2_scales', 'L0_ffn_fc2_bias', 'L0_c', 'L0_wmod']


def kernel(**inputs):
    import numpy as np
    import concourse.bacc as bacc
    from concourse.bass_utils import run_bass_kernel_spmd

    arrays = {name: np.ascontiguousarray(inputs[name]) for name in _INS}
    arrays["L0_attn_Wq"] = np.ascontiguousarray(arrays["L0_attn_Wq"].transpose(0, 2, 1))
    arrays["L0_attn_Wp"] = np.ascontiguousarray(arrays["L0_attn_Wp"].T)
    for name in ("L0_c", "L0_ffn_ln_gamma", "L0_ffn_ln_beta", "L0_ffn_fc1_bias"):
        arrays[name] = np.ascontiguousarray(arrays[name].reshape(-1, P).T)
    arrays["eye"] = np.eye(P, dtype=np.float32)
    nc = bacc.Bacc("TRN2", target_bir_lowering=False, num_devices=1)
    args = [nc.dram_tensor(name, a.shape, mybir.dt.from_np(a.dtype), kind="ExternalInput").ap() for name, a in arrays.items()]
    out = nc.dram_tensor("out", (1, N, D), F32, kind="ExternalOutput").ap()
    adaln_layer(nc, *args, out)
    result = run_bass_kernel_spmd(nc, [arrays], core_ids=[0])
    return result.results[0]["out"]
```

```python
from contextlib import ExitStack

import concourse.bass as bass
from concourse import mybir

F32, BF16, I32 = mybir.dt.float32, mybir.dt.bfloat16, mybir.dt.int32
ALU = mybir.AluOpType
ACT = mybir.ActivationFunctionType
AX = mybir.AxisListType

P = 128
BANK = 512
N, D = 4096, 256
H, E = 16, 16
F = 1024
EPS = 1e-5
TILES = N // P
DC = D // P
FT = F // P
GT = BANK // P
G = N // BANK
ROWS = 6 * E
STACK = ROWS + 3
NCH = H * G
PAIRS = TILES // 2
UNITS = TILES // 4
S_RING, P_RING, LAG = 3, 8, 2
REACH = 120.0


class Scope:

    def __init__(self, ctx, nc, stage):
        self.nc, self.stage, self.stack = nc, stage, ctx.enter_context(ExitStack())

    def take(self, name, words):
        return self.stack.enter_context(self.nc.sbuf_tensor(f"{self.stage}_{name}", [P, words], F32))[:, :]

    def banks(self, name, n):
        return self.stack.enter_context(self.nc.psum_tensor(f"{self.stage}_{name}", [P, n, BANK], F32))[:, :, :]

    def close(self):
        self.stack.close()


def wait(eng, semaphore, value):
    if not isinstance(value, int) or value > 0:
        eng.wait_ge(semaphore, value)


def rounds(eng, body, n):
    body(0)
    with eng.Fori(1, n) as i:
        body(i)


RSQRT_STEPS = 12


def rsqrt(dve, y, v, work, step, n):
    shifted, square = work[:, 0, :], work[:, 1, :]
    v_eps = work[:, 2, :]
    k = n * RSQRT_STEPS
    dve.tensor_scalar(v_eps, v, EPS, None, ALU.add).then_inc(step, 1)
    dve.wait_ge(step, k + 1)
    dve.tensor_scalar(shifted.bitcast(I32), v_eps.bitcast(I32), 1, None, ALU.logical_shift_right).then_inc(step, 1)
    dve.wait_ge(step, k + 2)
    dve.tensor_scalar(y.bitcast(I32), shifted.bitcast(I32), -1.0, float(0x5F3759DF), ALU.mult, ALU.add).then_inc(step, 1)
    for i in range(3):
        dve.wait_ge(step, k + (3 + 3 * i))
        dve.tensor_tensor(square, y, y, ALU.mult).then_inc(step, 1)
        dve.wait_ge(step, k + (4 + 3 * i))
        dve.scalar_tensor_tensor(out=square, in0=square, scalar=-0.5, in1=v_eps, op0=ALU.mult, op1=ALU.mult).then_inc(step, 1)
        dve.wait_ge(step, k + (5 + 3 * i))
        dve.scalar_tensor_tensor(out=y, in0=square, scalar=1.5, in1=y, op0=ALU.add, op1=ALU.mult).then_inc(step, 1)
    dve.wait_ge(step, k + RSQRT_STEPS)


def adaln_layer(nc, x, wq_t, wp_t, bp, gamma, beta, fc1_q, fc1_s, fc1_b, fc2_q, fc2_s, fc2_b,
                c_in, wmod, eye, out):
    ctx = ExitStack()

    def sb(name, shape, dt=F32):
        return ctx.enter_context(nc.sbuf_tensor(name, shape, dt))

    def sem(name):
        return ctx.enter_context(nc.semaphore(name))

    with ctx:
        parts_dram = nc.dram_tensor("parts_dram", [3, D, N], BF16, kind="Internal").ap()
        shift_dram = nc.dram_tensor("shift_dram", [P, 3, BANK], BF16, kind="Internal").ap()

        ident = sb("ident", [P, P])
        values = sb("values", [P, TILES, D])
        att = sb("att", [P, TILES, D])
        w1 = sb("w1", [P, DC, F])
        w2 = sb("w2", [P, FT, D])
        wp = sb("wp", [P, DC, D])
        mod = sb("mod", [P, 6, D])
        mod_col = sb("mod_col", [P, 4])
        bp_ga = sb("bp_ga", [P, D])
        b2_gb = sb("b2_gb", [P, D])
        gamma_col = sb("gamma_col", [P, DC])
        beta_col = sb("beta_col", [P, DC])
        b1_col = sb("b1_col", [P, FT])
        norms = sb("norms", [P, TILES, H])
        shifts = sb("shifts", [P, TILES, H])
        carried = sb("carried", [P, 2])

        def carry(pool):
            pool.tensor_tensor(carried[:, 1:2], ident[:, 0:1], ident[:, 0:1], ALU.mult)


        a = Scope(ctx, nc, "start")
        wmod_sb = a.take("wmod_sb", DC * 6 * D).rearrange("p (k m) -> p k m", k=DC)
        w1_int = w1[:, :, :].bitcast(I32)
        att_flat = att[:, :, :].rearrange("p t d -> p (t d)")
        w1_scale = att_flat[:, 0:DC * F].rearrange("p (k f) -> p k f", k=DC)
        w2_scale = att_flat[:, DC * F:DC * F + FT * D].rearrange("p (k f) -> p k f", k=FT)
        gates_at = DC * F + FT * D
        sign = att_flat[:, gates_at:gates_at + 2 * D].rearrange("p (s d) -> p s d", s=2)
        negated = att_flat[:, gates_at + 2 * D:gates_at + 4 * D].rearrange("p (s d) -> p s d", s=2)
        w2_int = w2[:, :, :].bitcast(I32)
        x_in = a.take("x_in", TILES * D).rearrange("p (t d) -> p t d", d=D)
        z_tok = a.take("z_tok", GT * D).rearrange("p (t d) -> p t d", t=GT)
        h_feat = a.take("h_feat", DC * BANK).rearrange("p (k n) -> p k n", k=DC)
        q_parts = a.take("q_parts", 3 * DC * BANK).bitcast(BF16).rearrange("p (r s k n) -> p r s (k n)", r=2, s=3, k=DC)
        q_rest = a.take("q_rest", 2 * DC * BANK).rearrange("p (r n) -> p r n", r=2)
        q_sq = a.take("q_sq", GT * D)
        wq_diag = a.take("wq_diag", DC * P).rearrange("p (k m) -> p k m", k=DC)
        silu_c = a.take("silu_c", 4 * DC).rearrange("p (s k) -> p s k", s=4)
        silu_wide = a.take("silu_wide", DC * P).rearrange("p (k m) -> p k m", k=DC)
        ones = a.take("ones", P)
        stats = a.take("stats", GT * 6).rearrange("p (t s) -> p t s", t=GT)
        moments = a.take("moments", GT * 2).rearrange("p (t s) -> p t s", t=GT)
        rstd = a.take("rstd", GT)
        rsqrt_work = a.take("rsqrt_work", 3 * GT).rearrange("p (s t) -> p s t", s=3)
        carrier = a.take("carrier", 1)

        def part_of(g, s):
            return q_parts[:, bass.ds(g % 2, 1), s, :].rearrange("p a n -> p (a n)")

        def rest_of(g):
            return q_rest[:, bass.ds(g % 2, 1), :].rearrange("p a n -> p (a n)")

        x_v = x[0].rearrange("(t p) d -> p t d", p=P)
        out_v = out[0].rearrange("(t p) d -> p t d", p=P)

        const_in, c_loaded, wmod_in, weights_in = sem("const_in"), sem("c_loaded"), sem("wmod_in"), sem("weights_in")
        wq_in, x0_loaded, x_loaded, diag_zero = sem("wq_in"), sem("x0_loaded"), sem("x_loaded"), sem("diag_zero")
        c_exp, c_step, wide_ready, mod_mm, mod_copied = sem("c_exp"), sem("c_step"), sem("wide_ready"), sem("mod_mm"), sem("mod_copied")
        col_mm, col_ready, mod_step, w_step = sem("col_mm"), sem("col_ready"), sem("mod_step"), sem("w_step")
        stats_done, moments_done, rstd_done, z_ready = sem("stats_done"), sem("moments_done"), sem("rstd_done"), sem("z_ready")
        z_turned, h_ready, q_feat_mm, q_tok_mm = sem("z_turned"), sem("h_ready"), sem("q_feat_mm"), sem("q_tok_mm")
        part_a, rest_ab, part_b, part_c, parts_stored = sem("part_a"), sem("rest_ab"), sem("part_b"), sem("part_c"), [sem("parts_stored0"), sem("parts_stored1")]
        v_copied, sq_ready, norms_ready = sem("v_copied"), sem("sq_ready"), sem("norms_ready")

        ps_turn = a.banks("turn", 2)
        ps_qf = a.banks("q_feat", 2)
        ps_qt = a.banks("q_tok", 2)
        ps_mod = a.banks("mod", 1)[:, 0, :]
        ps_col = a.banks("col", 1)[:, 0, 0:4]

        with nc.Block() as block:

            @block.sync
            def _(sp):
                sp.dma_start(silu_c[:, 0, :], c_in).then_inc(c_loaded, 16)
                sp.dma_start(wmod_sb, wmod.rearrange("(k p) m -> p k m", p=P)).then_inc(wmod_in, 16)
                sp.dma_start(x_in[:, 0:GT, :], x_v[:, 0:GT, :]).then_inc(x0_loaded, 16)
                sp.dma_start(ident[:, :], eye).then_inc(const_in, 16)
                sp.wait_ge(diag_zero, 1)
                for h in range(H):
                    k, r = divmod(h, H // DC)
                    sp.dma_start(wq_diag[E * r:E * r + E, k, E * r:E * r + E], wq_t[h]).then_inc(wq_in, 16)
                for g in range(1, G):
                    sp.dma_start(x_in[:, GT * g:GT * g + GT, :], x_v[:, GT * g:GT * g + GT, :]).then_inc(x_loaded, 16)
                sp.dma_start(w1_int, fc1_q.rearrange("(k p) f -> p k f", p=P)).then_inc(weights_in, 16)
                sp.dma_start(w2_int, fc2_q.rearrange("(k p) f -> p k f", p=P)).then_inc(weights_in, 16)
                sp.dma_start(wp[:, :, :], wp_t.rearrange("(k p) f -> p k f", p=P)).then_inc(weights_in, 16)
                sp.dma_start(w1_scale, fc1_s.partition_broadcast(P)).then_inc(weights_in, 16)
                sp.dma_start(w2_scale, fc2_s.partition_broadcast(P)).then_inc(weights_in, 16)
                sp.dma_start(bp_ga[:, :], bp.partition_broadcast(P)).then_inc(weights_in, 16)
                sp.dma_start(b2_gb[:, :], fc2_b.partition_broadcast(P)).then_inc(weights_in, 16)
                sp.dma_start(gamma_col[:, :], gamma).then_inc(weights_in, 16)
                sp.dma_start(beta_col[:, :], beta).then_inc(weights_in, 16)
                sp.dma_start(b1_col[:, :], fc1_b).then_inc(weights_in, 16)
                def store_parts(b):
                    for r in range(2):
                        g = b * 2 + r
                        sp.wait_ge(part_c, g + 1)
                        for k in range(DC):
                            sp.dma_start(parts_dram[:, k * P:(k + 1) * P, bass.ds(g * BANK, BANK)].rearrange("s p n -> p s n"),
                                         q_parts[:, r, :, k * BANK:(k + 1) * BANK]).then_inc(parts_stored[r], 16)

                rounds(sp, store_parts, G // 2)
                for r in range(2):
                    sp.wait_ge(parts_stored[r], 16 * DC * (G // 2))
                sp.wait_ge(weights_in, 160)

            @block.gpsimd
            def _(pool):
                pool.memset(wq_diag, 0.0).then_inc(diag_zero, 1)
                pool.memset(ones, 1.0).then_inc(c_step, 1)
                pool.wait_ge(const_in, 16)
                def small_parts(g):
                    pool.wait_ge(rest_ab, g + 1)
                    carry(pool)
                    pool.tensor_copy(part_of(g, 1), rest_of(g)).then_inc(part_b, 1)
                    pool.wait_ge(part_b, g + 1)
                    pool.tensor_tensor(part_of(g, 2), rest_of(g), part_of(g, 1), ALU.subtract).then_inc(part_c, 1)

                rounds(pool, small_parts, G)
            @block.scalar
            def _(act):
                act.wait_ge(c_loaded, 16)
                act.activation(silu_c[:, 1, :], silu_c[:, 0, :], ACT.Exp, scale=-1.0).then_inc(c_exp, 1)
                for i in range(3):
                    act.wait_ge(mod_mm, i + 1)
                    act.activation(mod[:, 2 * i:2 * i + 2, :], ps_mod.rearrange("p (s d) -> p s d", s=2), ACT.Copy).then_inc(mod_copied, 1)
                act.wait_ge(col_ready, 2)
                def evacuate(b, r):
                    g = b * 2 + r
                    act.wait_ge(z_turned, g + 1)
                    wait(act, q_tok_mm, g)
                    for k in range(DC):
                        last = act.activation(h_feat[:, k, :], ps_turn[:, k, :], ACT.Identity,
                                              bias=mod_col[:, k:k + 1], scale=mod_col[:, 2 + k:3 + k])
                    last.then_inc(h_ready, 1)
                    act.wait_ge(q_feat_mm, g + 1)
                    wait(act, parts_stored[r], b * (16 * DC))
                    act.activation(part_of(g, 0), ps_qf.rearrange("p k n -> p (k n)"), ACT.Copy, scale=2.0).then_inc(part_a, 1)
                    act.wait_ge(q_tok_mm, g + 1)
                    act.activation(values[:, bass.ds(g * GT, GT), :],
                                   ps_qt.rearrange("p b (t d) -> p (b t) d", d=D), ACT.Copy).then_inc(v_copied, 1)
                    wait(act, norms_ready, g)
                    act.activation(q_sq, ps_qt.rearrange("p b n -> p (b n)"), ACT.Square).then_inc(sq_ready, 1)

                def pair(b):
                    evacuate(b, 0)
                    evacuate(b, 1)

                rounds(act, pair, G // 2)
            @block.tensor
            def _(pe):
                pe.wait_ge(wide_ready, 1)
                pe.wait_ge(wmod_in, 16)
                for i in range(3):
                    if i:
                        pe.wait_ge(mod_copied, i)
                    for k in range(DC):
                        last = pe.matmul(ps_mod, silu_wide[:, k, :], wmod_sb[:, k, i * BANK:(i + 1) * BANK],
                                         start=(k == 0), stop=(k == DC - 1))
                    last.then_inc(mod_mm, 1)
                for j in range(4):
                    for k in range(DC):
                        last = pe.matmul(ps_col[:, j:j + 1], wmod_sb[:, k, j * P:(j + 1) * P], silu_c[:, 3, k:k + 1],
                                         start=(k == 0), stop=(k == DC - 1))
                last.then_inc(col_mm, 1)
                pe.wait_ge(const_in, 16)
                pe.wait_ge(wq_in, 16 * H)
                def queries(g):
                    pe.wait_ge(z_ready, g + 1)
                    wait(pe, h_ready, g)
                    for k in range(DC):
                        for t in range(GT):
                            last = pe.transpose(ps_turn[:, k, t * P:(t + 1) * P], z_tok[:, t, k * P:(k + 1) * P], ident[:, :])
                    last.then_inc(z_turned, 1)
                    pe.wait_ge(h_ready, g + 1)
                    wait(pe, rest_ab, g)
                    for k in range(DC):
                        last = pe.matmul(ps_qf[:, k, :], wq_diag[:, k, :], h_feat[:, k, :], start=True, stop=True)
                    last.then_inc(q_feat_mm, 1)
                    wait(pe, sq_ready, g)
                    for t in range(GT):
                        for k in range(DC):
                            col = (t % 2) * D + k * P
                            last = pe.matmul(ps_qt[:, t // 2, col:col + P], h_feat[:, k, t * P:(t + 1) * P], wq_diag[:, k, :],
                                             start=True, stop=True)
                    last.then_inc(q_tok_mm, 1)

                rounds(pe, queries, G)
            @block.vector
            def _(dve):
                dve.wait_ge(c_exp, 1)
                dve.tensor_scalar(silu_c[:, 2, :], silu_c[:, 1, :], 1.0, None, ALU.add).then_inc(c_step, 1)
                dve.wait_ge(c_step, 2)
                dve.reciprocal(silu_c[:, 1, :], silu_c[:, 2, :]).then_inc(c_step, 1)
                dve.wait_ge(c_step, 3)
                dve.tensor_tensor(silu_c[:, 3, :], silu_c[:, 0, :], silu_c[:, 1, :], ALU.mult).then_inc(c_step, 1)
                dve.wait_ge(c_step, 4)
                for k in range(DC):
                    last = dve.tensor_scalar(silu_wide[:, k, :], ones, silu_c[:, 3, k:k + 1], None, ALU.mult)
                last.then_inc(wide_ready, 1)

                def normalise(g):
                    for t in range(GT):
                        last = dve.bn_stats(stats[:, t, :], x_in[:, bass.ds(g * GT + t, 1), :].rearrange("p a d -> p (a d)"))
                    last.then_inc(stats_done, 1)
                    dve.wait_ge(stats_done, g + 1)
                    dve.memset(carrier, 0.0)
                    for t in range(GT):
                        last = dve.bn_aggr(moments[:, t, :], stats[:, t, :])
                    last.then_inc(moments_done, 1)
                    dve.wait_ge(moments_done, g + 1)
                    rsqrt(dve, rstd, moments[:, :, 1], rsqrt_work, rstd_done, g)
                    wait(dve, z_turned, g)
                    for t in range(GT):
                        last = dve.tensor_scalar(z_tok[:, t, :], x_in[:, bass.ds(g * GT + t, 1), :].rearrange("p a d -> p (a d)"),
                                                 moments[:, t, 0:1], rstd[:, t:t + 1], ALU.subtract, ALU.mult)
                    last.then_inc(z_ready, 1)

                def split_and_norms(g):
                    dve.wait_ge(part_a, g + 1)
                    if not isinstance(g, int) or g > 1:
                        dve.wait_ge(part_c, g - 1)
                    dve.scalar_tensor_tensor(out=rest_of(g), in0=ps_qf.rearrange("p k n -> p (k n)"), scalar=2.0, in1=part_of(g, 0),
                                             op0=ALU.mult, op1=ALU.subtract).then_inc(rest_ab, 1)
                    dve.wait_ge(sq_ready, g + 1)
                    dve.tensor_reduce(norms[:, bass.ds(g * GT, GT), :], q_sq.rearrange("p (t h e) -> p t h e", t=GT, h=H),
                                      AX.X, ALU.add).then_inc(norms_ready, 1)

                dve.wait_ge(x0_loaded, 16)
                normalise(0)
                dve.wait_ge(col_mm, 1)
                dve.tensor_copy(mod_col[:, 0:2], ps_col[:, 0:2]).then_inc(col_ready, 1)
                dve.tensor_scalar(mod_col[:, 2:4], ps_col[:, 2:4], 1.0, None, ALU.add).then_inc(col_ready, 1)
                dve.wait_ge(x_loaded, 16 * (G - 1))
                def both(g):
                    normalise(g + 1)
                    split_and_norms(g)

                both(0)
                both(1)
                with dve.Fori(2, G - 1) as g:
                    both(g)
                split_and_norms(G - 1)

        a.close()
        late = Scope(ctx, nc, "late")
        x_res = late.take("x_res", TILES * D).rearrange("p (t d) -> p t d", d=D)
        shared = late.take("att_now", GT * D)
        att_now = shared.rearrange("p (t d) -> p t d", t=GT)
        xr_in, xb_ready, att_copied = sem("xr_in"), sem("xb_ready"), sem("att_copied")
        stacks = Scope(ctx, nc, "stacks")
        stack_k = stacks.take("stack_k", N).bitcast(BF16).rearrange("p (b n) -> p b n", b=2)
        stack_q = stacks.take("stack_q", N).bitcast(BF16).rearrange("p (b n) -> p b n", b=2)
        a = Scope(ctx, nc, "shift")
        top_by_head = a.take("top_by_head", 1)
        top_diag = a.take("top_diag", H)
        top_wide = a.take("top_wide", H)
        ones16 = a.take("ones16", P)
        peak = a.take("peak", 1)
        fits = a.take("fits", 1).bitcast(I32)
        half_max = a.take("half_max", 2 * TILES).rearrange("p (t s) -> p t s", t=TILES)
        shift_now = a.take("shift_now", TILES * H)
        shift_rest = a.take("shift_rest", BANK)
        shift_parts = a.take("shift_parts", 3 * BANK // 2).bitcast(BF16).rearrange("p (s n) -> p s n", s=3)

        top_step, top_turned, top_bc, guess_step, fits_ready = (sem(n) for n in (
            "top_step", "top_turned", "top_bc", "guess_step", "fits_ready"))
        minus_set, root_done, stacks_in = sem("minus_set"), sem("root_done"), sem("stacks_in")
        max_stacks, row_scores, head_max = sem("max_stacks"), sem("row_scores"), sem("head_max")
        half_free = [sem("half_free0"), sem("half_free1")]
        shift_set, shift_turned, split_step, shift_stored = (sem(n) for n in (
            "shift_set", "shift_turned", "split_step", "shift_stored"))

        def load_stacks(eng, head, slot, done):
            rows = bass.ds(head * E, E)

            def put(stack, first, parts, src):
                dst = stack[first * E:(first + parts) * E, bass.ds(slot, 1), :].rearrange("s a n -> s (a n)")
                eng.dma_start(dst, src).then_inc(done, 16)

            def part(s, times):
                return parts_dram[s:s + 1, rows, :].broadcast_to([times, E, N])

            put(stack_k, 0, 3, part(0, 3))
            put(stack_k, 3, 2, part(1, 2))
            put(stack_k, 5, 1, part(2, 1))
            put(stack_q, 0, 3, parts_dram[:, rows, :])
            put(stack_q, 3, 2, parts_dram[0:2, rows, :])
            put(stack_q, 5, 1, part(0, 1))

        def load_shift(eng, head, slot, done):
            src = shift_dram.rearrange("(t h) s (o n) -> s h o t n", h=H, n=P)
            for part in range(3):
                eng.dma_start(stack_q[ROWS + part:ROWS + part + 1, bass.ds(slot, 1), :].rearrange("s a n -> s (a n)"),
                              src[part:part + 1, bass.ds(head, 1), :, :, :]).then_inc(done, 16)

        FILL, FILL_SHIFT = 16 * 6, 16 * 3
        FILL_ALL = FILL + FILL_SHIFT
        ps_half = [a.banks("half0", 4), a.banks("half1", 4)]
        turned = ps_half[0][:, 0, :]

        with nc.Block() as block:

            @block.sync
            def _(sp):
                sp.wait_ge(fits_ready, 1)
                with sp.If(sp.value_load(fits[0:1, 0:1], min_val=0, max_val=1) == 0):
                    load_stacks(sp, 0, 0, max_stacks)
                    sp.wait_ge(max_stacks, FILL)
                    load_stacks(sp, 1, 1, max_stacks)
                    with sp.Fori(2, H) as h:
                        sp.wait_ge(row_scores, (h - 1) * (2 * TILES) + 1)
                        load_stacks(sp, h, h % 2, max_stacks)
                    sp.wait_ge(max_stacks, FILL * H)
                sp.wait_ge(shift_set, 1)
                load_stacks(sp, 0, 0, stacks_in)
                sp.wait_ge(split_step, 5)
                sp.dma_start(shift_dram, shift_parts).then_inc(shift_stored, 16)
                sp.wait_ge(shift_stored, 16)
                load_shift(sp, 0, 0, stacks_in)
                sp.wait_ge(stacks_in, FILL_ALL)

            @block.tensor
            def _(pe):
                pe.wait_ge(top_step, 2)
                pe.transpose(turned[0:H, 0:P], top_wide, ident[:, :]).then_inc(top_turned, 1)
                pe.wait_ge(top_step, 4)
                pe.matmul(ps_half[0][:, 1, 0:H], ones16[0:H, :], top_diag[0:H, :], start=True, stop=True).then_inc(top_bc, 1)
                pe.wait_ge(fits_ready, 1)
                with pe.If(pe.value_load(fits[0:1, 0:1], min_val=0, max_val=1) == 0):
                    with pe.Fori(0, H) as h:
                        with pe.Fori(0, TILES) as t:
                            pe.wait_ge(max_stacks, (h + 1) * FILL)
                            for half in range(2):
                                pe.wait_ge(half_free[half], h * TILES + (t + 1))
                                for j in range(4 * half, 4 * half + 4):
                                    last = pe.matmul(ps_half[half][:, j % 4, :],
                                                     stack_k[0:ROWS, bass.ds(h % 2, 1), bass.ds(t * P, P)].rearrange("p a n -> p (a n)"),
                                                     stack_q[0:ROWS, bass.ds(h % 2, 1), j * BANK:(j + 1) * BANK].rearrange("p a n -> p (a n)"),
                                                     start=True, stop=True)
                                last.then_inc(row_scores, 1)
                pe.wait_ge(shift_set, 1)
                for o in range(4):
                    last = pe.transpose(turned[:, o * P:(o + 1) * P], shift_now[:, o * P:(o + 1) * P], ident[:, :])
                last.then_inc(shift_turned, 1)

            @block.gpsimd
            def _(pool):
                pool.memset(ones16, 1.0).then_inc(top_step, 1)
                pool.wait_ge(top_step, 1)
                pool.memset(stack_k[ROWS:STACK, :, :], -1.0).then_inc(minus_set, 1)
                pool.wait_ge(minus_set, 1)

            @block.scalar
            def _(act):
                act.wait_ge(guess_step, 1)
                act.activation(shifts[:, :, :], shifts[:, :, :], ACT.Sqrt, scale=4.0).then_inc(root_done, 1)

            @block.vector
            def _(dve):
                dve.wait_ge(top_step, 1)
                dve.tensor_reduce(top_wide, norms[:, :, :].rearrange("p t h -> p h t"), AX.X, ALU.max).then_inc(top_step, 1)
                dve.wait_ge(top_turned, 1)
                dve.tensor_reduce(top_by_head[0:H, :], turned[0:H, 0:P], AX.X, ALU.max).then_inc(top_step, 1)
                dve.wait_ge(top_step, 3)
                dve.tensor_scalar(top_diag[0:H, :], ident[0:H, 0:H], top_by_head[0:H, 0:1], None, ALU.mult).then_inc(top_step, 1)
                dve.wait_ge(top_bc, 1)
                dve.tensor_copy(top_wide, ps_half[0][:, 1, 0:H]).then_inc(top_step, 1)
                dve.wait_ge(top_step, 5)
                dve.tensor_tensor(shifts[:, :, :], norms[:, :, :], top_wide.unsqueeze(1).broadcast_to([P, TILES, H]), ALU.mult).then_inc(guess_step, 1)
                dve.tensor_reduce(peak, top_wide, AX.X, ALU.max).then_inc(top_step, 1)
                dve.wait_ge(top_step, 6)
                dve.tensor_scalar(fits, peak, REACH, None, ALU.is_le).then_inc(fits_ready, 1)
                dve.wait_ge(root_done, 1)
                dve.scalar_tensor_tensor(out=shifts[:, :, :], in0=norms[:, :, :], scalar=2.0, in1=shifts[:, :, :],
                                         op0=ALU.mult, op1=ALU.add).then_inc(guess_step, 1)
                dve.wait_ge(guess_step, 2)
                dve.wait_ge(fits_ready, 1)
                with dve.If(dve.value_load(fits[0:1, 0:1], min_val=0, max_val=1) == 0):
                    for half in range(2):
                        dve.memset(half_max[:, :, half:half + 1], 0.0).then_inc(half_free[half], 1)
                    with dve.Fori(0, H) as h:
                        with dve.Fori(0, TILES) as t:
                            for half in range(2):
                                dve.wait_ge(row_scores, h * (2 * TILES) + t * 2 + (half + 1))
                                dve.tensor_reduce(half_max[:, bass.ds(t, 1), half:half + 1], ps_half[half],
                                                  AX.XY, ALU.max).then_inc(half_free[half], 1)
                        for half in range(2):
                            dve.wait_ge(half_free[half], h * TILES + (TILES + 1))
                        dve.tensor_reduce(shifts[:, :, bass.ds(h, 1)], half_max, AX.X, ALU.max).then_inc(head_max, 1)
                        dve.wait_ge(head_max, h + 1)
                dve.tensor_copy(shift_now, shifts[:, :, :].rearrange("p t h -> p (t h)")).then_inc(shift_set, 1)
                dve.wait_ge(shift_turned, 1)
                dve.tensor_copy(shift_parts[:, 0, :], turned).then_inc(split_step, 1)
                dve.wait_ge(split_step, 1)
                dve.tensor_tensor(shift_rest, turned, shift_parts[:, 0, :], ALU.subtract).then_inc(split_step, 1)
                dve.wait_ge(split_step, 2)
                dve.tensor_copy(shift_parts[:, 1, :], shift_rest).then_inc(split_step, 1)
                dve.wait_ge(split_step, 3)
                dve.tensor_tensor(shift_rest, shift_rest, shift_parts[:, 1, :], ALU.subtract).then_inc(split_step, 1)
                dve.wait_ge(split_step, 4)
                dve.tensor_copy(shift_parts[:, 2, :], shift_rest).then_inc(split_step, 1)

        a.close()
        a = Scope(ctx, nc, "attend")
        probs = [a.take(f"probs{i}", 2 * BANK).rearrange("p (b n) -> p b n", b=2) for i in range(P_RING)]
        v_now = [a.take("v_now0", TILES * 32), a.take("v_now1", TILES * 32), shared]
        v_now = [v.rearrange("p (t e) -> p t e", t=TILES) for v in v_now]
        sums_sb = a.take("sums_sb", BANK)
        inverse = a.take("inverse", GT)
        whole = a.take("whole", GT * (E + 1)).rearrange("p (t e) -> p t e", t=GT)
        v_filled, quarters_added = sem("v_filled"), sem("quarters_added")
        scores_ready, exps_done, units_done = sem("scores_ready"), sem("exps_done"), sem("units_done")
        v_ready, sums_copied, sums_turned, inverse_ready, chunk_done = (sem(n) for n in (
            "v_ready", "sums_copied", "sums_turned", "inverse_ready", "chunk_done"))
        ps_scores = [a.banks(f"scores{i}", 2) for i in range(S_RING)]
        ps_sums, ps_turned = a.banks("sums", 1)[:, 0, :], a.banks("turned", 1)[:, 0, :]

        def chunks(eng, body):
            body(0, 0)
            with eng.Fori(0, (NCH - 2) // 3) as b:
                for r in range(3):
                    body(b * 3 + (r + 1), (r + 1) % 3)
            body(NCH - 1, (NCH - 1) % 3)

        with nc.Block() as block:

            @block.sync
            def _(sp):
                load_shift(sp, 1, 1, stacks_in)
                load_stacks(sp, 1, 1, stacks_in)
                sp.dma_start(x_res, x_v).then_inc(xr_in, 16)
                with sp.Fori(2, H) as h:
                    sp.wait_ge(scores_ready, (h - 1) * (G * PAIRS) + 1)
                    load_shift(sp, h, h % 2, stacks_in)
                    load_stacks(sp, h, h % 2, stacks_in)
                sp.wait_ge(stacks_in, FILL_ALL * H)

            @block.gpsimd
            def _(pool):
                for i in range(3):
                    pool.memset(v_now[i], 0.0).then_inc(v_filled, 1)
                    pool.wait_ge(v_filled, 2 * i + 1)
                    pool.memset(v_now[i][:, :, E:E + 1], 1.0).then_inc(v_filled, 1)
                    pool.wait_ge(v_filled, 2 * i + 2)

                def copy_values(c, r):
                    if not isinstance(c, int) or c >= 3:
                        pool.wait_ge(v_ready, c)
                        pool.wait_ge(units_done, c * UNITS - 2 * UNITS)
                        carry(pool)
                    pool.tensor_copy(v_now[r][:, :, 0:E], values[:, :, bass.ds((c // G) * E, E)]).then_inc(v_ready, 1)

                copy_values(0, 0)
                copy_values(1, 1)
                copy_values(2, 2)
                pool.wait_ge(xr_in, 16)
                pool.wait_ge(w_step, 1)
                for g in range(G):
                    xr = x_res[:, g * GT:g * GT + GT, :]
                    pool.tensor_tensor(xr, xr, bp_ga[:, :].unsqueeze(1).broadcast_to([P, GT, D]), ALU.add).then_inc(xb_ready, 1)
                with pool.Fori(1, (NCH - 2) // 3) as b:
                    for r in range(3):
                        copy_values(b * 3 + r, r)
                copy_values(NCH - 2, (NCH - 2) % 3)
                copy_values(NCH - 1, (NCH - 1) % 3)
                pool.wait_ge(chunk_done, NCH - G + 1)
                pool.wait_ge(units_done, (NCH - 2) * UNITS)
                pool.wait_ge(v_ready, NCH)
                pool.tensor_copy(att_now, att[:, 0:GT, :]).then_inc(att_copied, 1)

            @block.scalar
            def _(act):
                def exps(c, r):
                    for k in range(PAIRS):
                        act.wait_ge(scores_ready, c * PAIRS + (k + 1))
                        slot = k % P_RING
                        if k % 2 == 0 and (not isinstance(c, int) or c or k >= P_RING):
                            act.wait_ge(units_done, c * UNITS + (k - P_RING) // 2 + 1)
                        act.activation(probs[slot], ps_scores[(r + k) % S_RING], ACT.Exp).then_inc(exps_done, 1)
                chunks(act, exps)

            @block.tensor
            def _(pe):
                pe.wait_ge(minus_set, 1)

                def scores(c, r, k):
                    if not isinstance(c, int) or c or k >= S_RING:
                        pe.wait_ge(exps_done, c * PAIRS + (k - S_RING + 1))
                    slot = bass.ds((c // G) % 2, 1)
                    for b in range(2):
                        t = 2 * k + b
                        last = pe.matmul(ps_scores[(r + k) % S_RING][:, b, :],
                                         stack_k[0:STACK, slot, t * P:(t + 1) * P].rearrange("p a n -> p (a n)"),
                                         stack_q[0:STACK, slot, bass.ds((c % G) * BANK, BANK)].rearrange("p a n -> p (a n)"),
                                         start=True, stop=True)
                    last.then_inc(scores_ready, 1)

                def weigh(c, r, u):
                    if u == 0:
                        pe.wait_ge(v_ready, c + 1)
                        if not isinstance(c, int) or c:
                            pe.wait_ge(sums_copied, c)
                    pe.wait_ge(exps_done, c * PAIRS + (2 * u + 2))
                    for q in range(4):
                        t = 4 * u + q
                        slot = (t // 2) % P_RING
                        last = pe.matmul(ps_sums[32 * q:32 * q + 32, :], v_now[r][:, t, :], probs[slot][:, t % 2, :],
                                         start=(u == 0), stop=(u == UNITS - 1))
                    last.then_inc(units_done, 1)

                def turn_sums(c):
                    pe.wait_ge(sums_copied, c + 1)
                    if not isinstance(c, int) or c:
                        pe.wait_ge(quarters_added, c)
                    for t in range(GT):
                        last = pe.transpose(ps_turned[:, t * P:(t + 1) * P], sums_sb[:, t * P:(t + 1) * P], ident[:, :])
                    last.then_inc(sums_turned, 1)

                def chunk(c, r):
                    head = c // G
                    pe.wait_ge(stacks_in, (head + 1) * FILL_ALL)
                    before = c - 1
                    for u in range(UNITS):
                        scores(c, r, 2 * u)
                        scores(c, r, 2 * u + 1)
                        if u >= LAG:
                            weigh(c, r, u - LAG)
                        elif not isinstance(c, int) or c:
                            weigh(before, (r - 1) % 3, u - LAG + UNITS)
                        if u == LAG + 1 and (not isinstance(c, int) or c):
                            turn_sums(before)

                chunks(pe, chunk)
                for u in range(UNITS - LAG, UNITS):
                    weigh(NCH - 1, (NCH - 1) % 3, u)
                turn_sums(NCH - 1)

            @block.vector
            def _(dve):
                def copy_sums(c):
                    dve.wait_ge(units_done, c * UNITS + UNITS)
                    if not isinstance(c, int) or c:
                        dve.wait_ge(sums_turned, c)
                    dve.tensor_copy(sums_sb, ps_sums).then_inc(sums_copied, 1)

                def divide(c):
                    dve.wait_ge(sums_turned, c + 1)
                    dve.tensor_reduce(whole, ps_turned.rearrange("p (t q e) -> p t e q", t=GT, q=4)[:, :, 0:E + 1, :],
                                      AX.X, ALU.add).then_inc(quarters_added, 1)
                    dve.wait_ge(quarters_added, c + 1)
                    dve.reciprocal(inverse, whole[:, :, E]).then_inc(inverse_ready, 1)
                    dve.wait_ge(inverse_ready, c + 1)
                    dve.tensor_tensor(att[:, bass.ds((c % G) * GT, GT), bass.ds((c // G) * E, E)], whole[:, :, 0:E],
                                      inverse.unsqueeze(2).broadcast_to([P, GT, E]), ALU.mult).then_inc(chunk_done, 1)

                dve.wait_ge(mod_copied, 3)
                gates = mod[:, 2:6:3, :]
                dve.tensor_scalar(sign, gates, 0.0, 2.0, ALU.is_ge, ALU.mult).then_inc(mod_step, 1)
                dve.tensor_scalar(negated, gates, -1.0, None, ALU.mult).then_inc(mod_step, 1)
                dve.wait_ge(mod_step, 2)
                dve.tensor_scalar(sign, sign, -1.0, None, ALU.add).then_inc(mod_step, 1)
                dve.tensor_tensor(negated, negated, gates, ALU.max).then_inc(mod_step, 1)
                dve.wait_ge(mod_step, 4)
                dve.scalar_tensor_tensor(out=gates, in0=negated, scalar=0.25, in1=sign, op0=ALU.max, op1=ALU.mult).then_inc(mod_step, 1)
                dve.tensor_scalar(mod[:, 4, :], mod[:, 4, :], 1.0, None, ALU.add).then_inc(mod_step, 1)
                dve.wait_ge(mod_step, 6)
                dve.tensor_scalar(sign[:, 0, :], mod[:, 5, :], 0.5, None, ALU.mult).then_inc(mod_step, 1)
                dve.wait_ge(mod_step, 7)
                dve.wait_ge(weights_in, 160)
                dve.tensor_tensor(bp_ga[:, :], bp_ga[:, :], mod[:, 2, :], ALU.mult).then_inc(w_step, 1)
                dve.tensor_tensor(b2_gb[:, :], b2_gb[:, :], sign[:, 0, :], ALU.mult).then_inc(w_step, 1)
                for k in range(DC):
                    dve.tensor_tensor(wp[:, k, :], wp[:, k, :], mod[:, 2, :], ALU.mult).then_inc(w_step, 1)
                dve.scalar_tensor_tensor(out=w1[:, :, :], in0=w1_int, scalar=-128.0, in1=w1_scale,
                                         op0=ALU.add, op1=ALU.mult).then_inc(w_step, 1)
                dve.scalar_tensor_tensor(out=w2[:, :, :], in0=w2_int, scalar=-128.0, in1=w2_scale,
                                         op0=ALU.add, op1=ALU.mult).then_inc(w_step, 1)
                dve.wait_ge(w_step, 6)
                for k in range(FT):
                    dve.tensor_tensor(w2[:, k, :], w2[:, k, :], sign[:, 0, :], ALU.mult).then_inc(w_step, 1)
                dve.wait_ge(w_step, 6 + FT)

                copy_sums(0)
                with dve.Fori(1, NCH) as c:
                    divide(c - 1)
                    copy_sums(c)
                divide(NCH - 1)
                dve.wait_ge(chunk_done, NCH)

        a.close()
        stacks.close()
        a = Scope(ctx, nc, "out")

        def tok(name):
            return a.take(name, GT * D).rearrange("p (t d) -> p t d", t=GT)

        x1, z1, hid, mix = tok("x1"), tok("z1"), tok("hid"), tok("mix")
        att_feat = a.take("att_feat", DC * BANK).rearrange("p (k n) -> p k n", k=DC)
        base = [tok("base0"), tok("base1")]
        y_out = [tok("y_out0"), tok("y_out1")]
        ps_turn, ps_proj, ps_down = a.banks("turn", 2), a.banks("proj", 2), a.banks("down", 2)
        ps_up = [a.banks("up0", 1)[:, 0, :], a.banks("up1", 1)[:, 0, :]]
        ffn_in = a.take("ffn_in", DC * BANK).rearrange("p (k n) -> p k n", k=DC)
        hidden = a.take("hidden", FT * BANK).rearrange("p (k n) -> p k n", k=FT)
        st2 = a.take("st2", GT * 6).rearrange("p (t s) -> p t s", t=GT)
        mo2 = a.take("mo2", 2 * GT * 2).rearrange("p (r t s) -> p r t s", r=2, t=GT)
        rs2 = a.take("rs2", 2 * GT).rearrange("p (r t) -> p r t", r=2)
        carrier2 = a.take("carrier2", 1)
        rsqrt_work2 = a.take("rsqrt_work2", 3 * GT).rearrange("p (s t) -> p s t", s=3)

        names = ("att_turned", "af_ready", "proj_mm", "x1_ready", "n_stats", "n_mom", "n_rstd",
                 "z1_ready", "scaled", "hid_ready", "mix_ready", "base_ready", "z2_ready", "z2_turned", "fi_ready",
                 "up_mm", "act_done", "down_mm", "y_ready")
        (att_turned, af_ready, proj_mm, x1_ready, n_stats, n_mom, n_rstd,
         z1_ready, scaled, hid_ready, mix_ready, base_ready, z2_ready, z2_turned, fi_ready,
         up_mm, act_done, down_mm, y_ready) = (sem(n) for n in names)
        y_stored = [sem("y_stored0"), sem("y_stored1")]
        z2 = z1

        def wide(v):
            return v.unsqueeze(1).broadcast_to([P, GT, D])

        with nc.Block() as block:

            @block.sync
            def _(sp):
                def store(b):
                    for r in range(2):
                        g = b * 2 + r
                        sp.wait_ge(y_ready, g + 1)
                        sp.dma_start(out_v[:, bass.ds(g * GT, GT), :], y_out[r]).then_inc(y_stored[r], 16)

                rounds(sp, store, G // 2)
                for r in range(2):
                    sp.wait_ge(y_stored[r], 16 * (G // 2))

            @block.gpsimd
            def _(pool):
                def copy_att(g):
                    pool.wait_ge(att_turned, g)
                    carry(pool)
                    pool.tensor_copy(att_now, att[:, bass.ds(g * GT, GT), :]).then_inc(att_copied, 1)

                def output_base(g, r):
                    pool.wait_ge(hid_ready, g + 1)
                    pool.tensor_tensor(mix, hid, wide(mod[:, 5, :]), ALU.mult).then_inc(mix_ready, 1)
                    pool.wait_ge(mix_ready, g * 3 + 1)
                    pool.tensor_tensor(mix, mix, wide(b2_gb[:, :]), ALU.add).then_inc(mix_ready, 1)
                    pool.wait_ge(mix_ready, g * 3 + 2)
                    if not isinstance(g, int) or g > 1:
                        pool.wait_ge(y_ready, g - 1)
                    pool.tensor_tensor(base[r], mix, x1, ALU.add).then_inc(mix_ready, 1)

                copy_att(1)
                output_base(0, 0)
                with pool.Fori(0, G // 2 - 1) as b:
                    for r in range(2):
                        copy_att(b * 2 + (r + 2))
                        output_base(b * 2 + (r + 1), (r + 1) % 2)
                output_base(G - 1, (G - 1) % 2)
            @block.scalar
            def _(act):
                def turn_att(g):
                    act.wait_ge(att_turned, g + 1)
                    wait(act, proj_mm, g)
                    act.activation(att_feat, ps_turn, ACT.Copy).then_inc(af_ready, 1)

                def turn_z2(g):
                    act.wait_ge(z2_turned, g + 1)
                    wait(act, up_mm, g * FT)
                    for k in range(DC):
                        last = act.activation(ffn_in[:, k, :], ps_turn[:, k, :], ACT.Identity,
                                              bias=beta_col[:, k:k + 1], scale=gamma_col[:, k:k + 1])
                    last.then_inc(fi_ready, 1)

                def silus(g):
                    for f in range(FT):
                        act.wait_ge(up_mm, g * FT + (f + 1))
                        if f == 0:
                            wait(act, down_mm, g)
                        act.activation(hidden[:, f, :], ps_up[f % 2], ACT.Silu, bias=b1_col[:, f:f + 1])\
                           .then_inc(act_done, 1)

                turn_att(0)
                turn_att(1)
                turn_z2(0)
                def step(g):
                    silus(g)
                    turn_att(g + 2)
                    turn_z2(g + 1)

                rounds(act, step, G - 2)
                silus(G - 2)
                turn_z2(G - 1)
                silus(G - 1)

            @block.tensor
            def _(pe):
                def turn_att(g):
                    pe.wait_ge(att_copied, g + 1)
                    if isinstance(g, int) and g < 2:
                        wait(pe, af_ready, g)
                    else:
                        pe.wait_ge(fi_ready, g - 1)
                    for k in range(DC):
                        for t in range(GT):
                            last = pe.transpose(ps_turn[:, k, t * P:(t + 1) * P], att_now[:, t, k * P:(k + 1) * P], ident[:, :])
                    last.then_inc(att_turned, 1)

                def project(g):
                    pe.wait_ge(af_ready, g + 1)
                    wait(pe, x1_ready, g)
                    for t in range(GT):
                        for k in range(DC):
                            last = pe.matmul(ps_proj[:, t // 2, (t % 2) * D:(t % 2 + 1) * D], att_feat[:, k, t * P:(t + 1) * P],
                                             wp[:, k, :], start=(k == 0), stop=(k == DC - 1))
                    last.then_inc(proj_mm, 1)

                def turn_z2(g):
                    pe.wait_ge(z2_ready, g + 1)
                    if isinstance(g, int) and g == G - 1:
                        pe.wait_ge(fi_ready, g)
                    else:
                        pe.wait_ge(af_ready, g + 2)
                    for k in range(DC):
                        for t in range(GT):
                            last = pe.transpose(ps_turn[:, k, t * P:(t + 1) * P], z2[:, t, k * P:(k + 1) * P], ident[:, :])
                    last.then_inc(z2_turned, 1)

                def up(g):
                    pe.wait_ge(fi_ready, g + 1)
                    for f in range(FT):
                        wait(pe, act_done, g * FT + max(f - 1, 0))
                        for k in range(DC):
                            last = pe.matmul(ps_up[f % 2], w1[:, k, f * P:(f + 1) * P], ffn_in[:, k, :],
                                             start=(k == 0), stop=(k == DC - 1))
                        last.then_inc(up_mm, 1)

                def down(g):
                    pe.wait_ge(act_done, g * FT + FT)
                    wait(pe, y_ready, g)
                    for t in range(GT):
                        for f in range(FT):
                            last = pe.matmul(ps_down[:, t // 2, (t % 2) * D:(t % 2 + 1) * D], hidden[:, f, t * P:(t + 1) * P],
                                             w2[:, f, :], start=(f == 0), stop=(f == FT - 1))
                    last.then_inc(down_mm, 1)

                turn_att(0)
                project(0)
                turn_att(1)
                turn_z2(0)
                def step(g):
                    project(g + 1)
                    up(g)
                    turn_att(g + 2)
                    down(g)
                    turn_z2(g + 1)

                rounds(pe, step, G - 2)
                project(G - 1)
                up(G - 2)
                down(G - 2)
                turn_z2(G - 1)
                up(G - 1)
                down(G - 1)

            @block.vector
            def _(dve):
                def stats_of(src, r, n):
                    for t in range(GT):
                        last = dve.bn_stats(st2[:, t, :], src[:, t, :])
                    last.then_inc(n_stats, 1)
                    dve.wait_ge(n_stats, n + 1)
                    dve.memset(carrier2, 0.0)
                    for t in range(GT):
                        last = dve.bn_aggr(mo2[:, r, t, :], st2[:, t, :])
                    last.then_inc(n_mom, 1)
                    dve.wait_ge(n_mom, n + 1)
                    rsqrt(dve, rs2[:, r, :], mo2[:, r, :, 1], rsqrt_work2, n_rstd, n)

                def middle(g):
                    dve.wait_ge(proj_mm, g + 1)
                    wait(dve, mix_ready, g * 3)
                    dve.tensor_tensor(x1, ps_proj.rearrange("p b (t d) -> p (b t) d", d=D), x_res[:, bass.ds(g * GT, GT), :],
                                      ALU.add).then_inc(x1_ready, 1)
                    dve.wait_ge(x1_ready, g + 1)
                    wait(dve, z2_turned, g)
                    stats_of(x1, 0, g * 2)
                    for t in range(GT):
                        last = dve.tensor_scalar(z1[:, t, :], x1[:, t, :], mo2[:, 0, t, 0:1], rs2[:, 0, t:t + 1], ALU.subtract, ALU.mult)
                    last.then_inc(z1_ready, 1)
                    dve.wait_ge(z1_ready, g + 1)
                    dve.tensor_tensor(hid, z1, wide(mod[:, 4, :]), ALU.mult).then_inc(scaled, 1)
                    dve.wait_ge(scaled, g + 1)
                    dve.tensor_tensor(hid, hid, wide(mod[:, 3, :]), ALU.add).then_inc(hid_ready, 1)
                    dve.wait_ge(hid_ready, g + 1)
                    stats_of(hid, 1, g * 2 + 1)
                    for t in range(GT):
                        last = dve.tensor_scalar(z2[:, t, :], hid[:, t, :], mo2[:, 1, t, 0:1], rs2[:, 1, t:t + 1], ALU.subtract, ALU.mult)
                    last.then_inc(z2_ready, 1)

                def finish(g, r, b):
                    dve.wait_ge(down_mm, g + 1)
                    dve.wait_ge(mix_ready, g * 3 + 3)
                    wait(dve, y_stored[r], b * 16)
                    dve.tensor_tensor(y_out[r], ps_down.rearrange("p b (t d) -> p (b t) d", d=D), base[r], ALU.add)\
                       .then_inc(y_ready, 1)

                dve.wait_ge(xb_ready, G)
                middle(0)
                def pair(b):
                    for r in range(2):
                        middle(b * 2 + (r + 1))
                        finish(b * 2 + r, r, b)

                rounds(dve, pair, G // 2 - 1)
                middle(G - 1)
                finish(G - 2, 0, G // 2 - 1)
                finish(G - 1, 1, G // 2 - 1)


_INS = ['L0_attn_x', 'L0_attn_Wq', 'L0_attn_Wp', 'L0_attn_bp', 'L0_ffn_ln_gamma', 'L0_ffn_ln_beta', 'L0_ffn_fc1_q',
        'L0_ffn_fc1_scales', 'L0_ffn_fc1_bias', 'L0_ffn_fc2_q', 'L0_ffn_fc2_scales', 'L0_ffn_fc2_bias', 'L0_c', 'L0_wmod']


def kernel(**inputs):
    import numpy as np
    import concourse.bacc as bacc
    from concourse.bass_utils import run_bass_kernel_spmd

    arrays = {name: np.ascontiguousarray(inputs[name]) for name in _INS}
    arrays["L0_attn_Wq"] = np.ascontiguousarray(arrays["L0_attn_Wq"].transpose(0, 2, 1))
    arrays["L0_attn_Wp"] = np.ascontiguousarray(arrays["L0_attn_Wp"].T)
    for name in ("L0_c", "L0_ffn_ln_gamma", "L0_ffn_ln_beta", "L0_ffn_fc1_bias"):
        arrays[name] = np.ascontiguousarray(arrays[name].reshape(-1, P).T)
    arrays["eye"] = np.eye(P, dtype=np.float32)
    nc = bacc.Bacc("TRN2", target_bir_lowering=False, num_devices=1)
    args = [nc.dram_tensor(name, a.shape, mybir.dt.from_np(a.dtype), kind="ExternalInput").ap() for name, a in arrays.items()]
    out = nc.dram_tensor("out", (1, N, D), F32, kind="ExternalOutput").ap()
    adaln_layer(nc, *args, out)
    result = run_bass_kernel_spmd(nc, [arrays], core_ids=[0])
    return result.results[0]["out"]
```
